# Optimizing a Trainium2 kernel written in Bass

```python
import numpy as np
import jax
import jax.numpy as jnp

def _softmax(x, axis=-1):
    return jax.nn.softmax(x, axis=axis)

def _gelu(x):
    return jax.nn.gelu(x, approximate=True)

def _silu(x):
    return jax.nn.silu(x)

def _sigmoid(x):
    return jax.nn.sigmoid(x)

def _layernorm(x, axis=-1, eps=1e-05):
    m = jnp.mean(x, axis=axis, keepdims=True)
    v = jnp.var(x, axis=axis, keepdims=True)
    return (x - m) / jnp.sqrt(v + eps)

def _scatter_add(tgt, idx, src, axis=0):
    return tgt.at[idx].add(src)

def _segment_sum(src, seg, n):
    return jax.ops.segment_sum(src, seg, n)
kernel_name = 'mk_prb_d1_jaxref_r8_6bd542'

def setup_inputs(seed: int=0):
    np.random.seed(seed)
    _w = jnp.asarray

    def _L0_attn_setup():
        import jax, jax.numpy as jnp
        import numpy as np
        import math
        EMBED_DIM = 128
        NDIM = 2
        SCALE = math.sqrt(1.0 / NDIM)

        def _ema_kernel(delta, alpha, beta, gamma, length):
            p = jax.nn.sigmoid(delta)
            a = jax.nn.sigmoid(alpha)
            q = 1.0 - p * a
            t = jnp.arange(length, dtype=q.dtype)
            vander = t[None, None, :] * jnp.log(q)
            kernel = p * beta * jnp.exp(vander)
            return jnp.einsum('dnl,dn->dl', kernel, gamma * SCALE)
        key = jax.random.key(seed)
        ks = jax.random.split(key, 6)
        B, S, D, N = (4, 1024, EMBED_DIM, NDIM)
        x = jax.random.normal(ks[0], (B, S, D), dtype=jnp.float32)
        delta = 0.2 * jax.random.normal(ks[1], (D, N, 1), dtype=jnp.float32)
        alpha = 0.2 * jax.random.normal(ks[2], (D, N, 1), dtype=jnp.float32)
        val = jnp.where(jnp.arange(N) % 2 == 1, -1.0, 1.0).reshape(N, 1).astype(jnp.float32)
        beta = 0.02 * jax.random.normal(ks[3], (D, N, 1), dtype=jnp.float32) + val
        gamma = jax.random.normal(ks[4], (D, N), dtype=jnp.float32)
        omega = jax.random.normal(ks[5], (D,), dtype=jnp.float32)
        return {'x': x, 'delta': delta, 'alpha': alpha, 'beta': beta, 'gamma': gamma, 'omega': omega}
    _L0_attn_in = _L0_attn_setup()

    def _L0_ffn_setup():
        import jax, jax.numpy as jnp
        import numpy as np
        B, S, H, F, E, R, TOPK = (4, 256, 128, 512, 4, 4, 2)

        def _more_forward(x, Wg, bg, W1, b1, W2, b2):
            b, s, h = x.shape
            cur = x
            for r in range(R):
                flat = cur.reshape(-1, h)
                logits = flat @ Wg[r] + bg[r]
                vals, idx = jax.lax.top_k(logits, TOPK)
                w = jax.nn.softmax(vals, axis=-1)
                cw = jnp.sum(jax.nn.one_hot(idx, E, dtype=flat.dtype) * w[..., None], axis=1)
                hmid = jax.nn.gelu(jnp.einsum('nh,ehf->enf', flat, W1) + b1[:, None, :])
                y = jnp.einsum('enf,efh->enh', hmid, W2) + b2[:, None, :]
                out = jnp.einsum('ne,enh->nh', cw, y)
                cur = cur + out.reshape(b, s, h)
            return cur
        key = jax.random.key(seed)
        ks = jax.random.split(key, 8)
        scale = 0.02
        return {'x': jax.random.normal(ks[0], (B, S, H), dtype=jnp.float32), 'Wg': jax.random.normal(ks[1], (R, H, E), dtype=jnp.float32) * scale, 'bg': jnp.zeros((R, E), dtype=jnp.float32), 'W1': jax.random.normal(ks[2], (E, H, F), dtype=jnp.float32) * scale, 'b1': jnp.zeros((E, F), dtype=jnp.float32), 'W2': jax.random.normal(ks[3], (E, F, H), dtype=jnp.float32) * scale, 'b2': jnp.zeros((E, H), dtype=jnp.float32)}
    _L0_ffn_in = _L0_ffn_setup()
    _d = {'L0_attn_x': _L0_attn_in['x'], 'L0_attn_delta': _L0_attn_in['delta'], 'L0_attn_alpha': _L0_attn_in['alpha'], 'L0_attn_beta': _L0_attn_in['beta'], 'L0_attn_gamma': _L0_attn_in['gamma'], 'L0_attn_omega': _L0_attn_in['omega'], 'L0_ffn_Wg': _L0_ffn_in['Wg'], 'L0_ffn_bg': _L0_ffn_in['bg'], 'L0_ffn_W1': _L0_ffn_in['W1'], 'L0_ffn_b1': _L0_ffn_in['b1'], 'L0_ffn_W2': _L0_ffn_in['W2'], 'L0_ffn_b2': _L0_ffn_in['b2']}
    _x0 = _d['L0_attn_x']
    _d['L0_attn_x'] = jax.random.normal(jax.random.fold_in(jax.random.key(seed), 1), (8, 512, 128), dtype=_x0.dtype)
    del _x0
    return _d

def reference(L0_attn_x, L0_attn_delta, L0_attn_alpha, L0_attn_beta, L0_attn_gamma, L0_attn_omega, L0_ffn_Wg, L0_ffn_bg, L0_ffn_W1, L0_ffn_b1, L0_ffn_W2, L0_ffn_b2):

    def _L0_attn_ref(x, delta, alpha, beta, gamma, omega):
        import jax, jax.numpy as jnp
        import numpy as np
        import math
        EMBED_DIM = 128
        NDIM = 2
        SCALE = math.sqrt(1.0 / NDIM)

        def _ema_kernel(delta, alpha, beta, gamma, length):
            p = jax.nn.sigmoid(delta)
            a = jax.nn.sigmoid(alpha)
            q = 1.0 - p * a
            t = jnp.arange(length, dtype=q.dtype)
            vander = t[None, None, :] * jnp.log(q)
            kernel = p * beta * jnp.exp(vander)
            return jnp.einsum('dnl,dn->dl', kernel, gamma * SCALE)
        B, S, D = x.shape
        residual = x * omega
        xt = jnp.transpose(x, (0, 2, 1))
        k = _ema_kernel(delta, alpha, beta, gamma, S)
        n = 2 * S
        k_f = jnp.fft.rfft(k.astype(jnp.float32), n=n)
        x_f = jnp.fft.rfft(xt.astype(jnp.float32), n=n)
        out = jnp.fft.irfft(x_f * k_f, n=n)[..., :S]
        out = out.astype(x.dtype)
        return jax.nn.silu(jnp.transpose(out, (0, 2, 1)) + residual)

    def _L0_ffn_ref(x, Wg, bg, W1, b1, W2, b2):
        import jax, jax.numpy as jnp
        import numpy as np
        B, S, H, F, E, R, TOPK = (4, 256, 128, 512, 4, 4, 2)

        def _more_forward(x, Wg, bg, W1, b1, W2, b2):
            b, s, h = x.shape
            cur = x
            for r in range(R):
                flat = cur.reshape(-1, h)
                logits = flat @ Wg[r] + bg[r]
                vals, idx = jax.lax.top_k(logits, TOPK)
                w = jax.nn.softmax(vals, axis=-1)
                cw = jnp.sum(jax.nn.one_hot(idx, E, dtype=flat.dtype) * w[..., None], axis=1)
                hmid = jax.nn.gelu(jnp.einsum('nh,ehf->enf', flat, W1) + b1[:, None, :])
                y = jnp.einsum('enf,efh->enh', hmid, W2) + b2[:, None, :]
                out = jnp.einsum('ne,enh->nh', cw, y)
                cur = cur + out.reshape(b, s, h)
            return cur
        return _more_forward(x, Wg, bg, W1, b1, W2, b2)
    x = L0_attn_x
    xn = _layernorm(x, axis=-1)
    x = x + _L0_attn_ref(xn, L0_attn_delta, L0_attn_alpha, L0_attn_beta, L0_attn_gamma, L0_attn_omega) + _L0_ffn_ref(xn, L0_ffn_Wg, L0_ffn_bg, L0_ffn_W1, L0_ffn_b1, L0_ffn_W2, L0_ffn_b2)
    return x

_drawn_inputs = setup_inputs


def setup_inputs(seed=0):
    import zlib

    import numpy as np

    out = dict(_drawn_inputs(seed))
    spreads = {'L0_ffn_bg': (0.0, 0.1), 'L0_ffn_b1': (0.0, 0.336), 'L0_ffn_b2': (0.0, 0.1)}
    factors = {'L0_attn_delta': 3.118, 'L0_attn_alpha': 3.766, 'L0_attn_beta': 8.0}
    for name, (base, spread) in spreads.items():
        noise = np.random.default_rng([zlib.crc32(name.encode()), seed]).standard_normal(out[name].shape)
        drawn = base * np.exp(spread * noise) if base else spread * noise
        out[name] = jnp.asarray(drawn.astype(out[name].dtype))
    for name, factor in factors.items():
        out[name] = (out[name] * factor).astype(out[name].dtype)
    return out
```

```python
from contextlib import ExitStack

import concourse.bass as bass
from concourse import mybir

F32 = mybir.dt.float32
F32R = mybir.dt.float32r
ALU = mybir.AluOpType
ACT = mybir.ActivationFunctionType
AX_X = mybir.AxisListType.X


def ema_and_routed_ffn_kernel(nc, x, delta, alpha, beta, gamma, omega, Wg, bg, W1, b1, W2, b2, out):
    B, T, H = x.shape
    R, _, E = Wg.shape
    F = W1.shape[2]
    N = delta.shape[1]
    P = 128
    FC = F // P
    STEPS = E * FC
    TILES = T // P
    NTILES = B * TILES
    PAIRS = B // 2
    SLOTS = B * R
    LAG = 3
    ZR = 4
    YR = 2
    TR = 4
    CH = B * T // (SLOTS // 2)
    HALVES = T // CH
    LN_EPS = 1e-05
    EMA_SCALE = (1.0 / N) ** 0.5
    ROWS = E * FC + E + 1
    assert H == P and T == 512 and SLOTS % 2 == 0 and HALVES == 2 and STEPS == 16
    HI_ON_DVE = (4, 11, 15)
    BROADCAST_AT = (0, 4, 8, 12)
    HI_ON_ACT = [j for j in range(STEPS) if j not in HI_ON_DVE]

    x_v = x.rearrange("b (t p) h -> b p t h", p=P)
    out_v = out.rearrange("b (t p) h -> b p t h", p=P)

    with ExitStack() as ctx:
        def sb(name, shape, dt=F32):
            return ctx.enter_context(nc.sbuf_tensor(name, shape, dt))

        def sem(name):
            return ctx.enter_context(nc.semaphore(name))

        x_tok = sb("x_tok", [P, NTILES, H])
        xn_T = sb("xn_T", [P, B * T])
        state = sb("state", [P, B * T])
        attn_T = sb("attn_T", [P, B * T])
        xn_tok = attn_T[:].rearrange("p (b t h) -> p b t h", b=B, t=TILES)
        w1_raw = sb("w1_raw", [P, E, F])
        w2_raw = sb("w2_raw", [P, E, FC, H])
        w1_hi = sb("w1_hi", [P, E, F], F32R)
        w1_lo = sb("w1_lo", [P, E, F], F32R)
        w2_hi = sb("w2_hi", [P, E, FC, H], F32R)
        w2_lo = sb("w2_lo", [P, E, FC, H], F32R)
        wg_raw = sb("wg_raw", [P, R, E])
        wg_split = sb("wg_split", [P, R, 2, E], F32R)
        bg_bc = sb("bg_bc", [P, R, E])
        rows = sb("rows", [ROWS, P])
        cols = sb("cols", [P, ROWS])
        cur_hi = sb("cur_hi", [P, 2, T], F32R)
        cur_lo = sb("cur_lo", [P, 2, T], F32R)
        h_hi = sb("h_hi", [P, ZR, T], F32R)
        h_lo = sb("h_lo", [P, ZR, T], F32R)
        lg = sb("lg", [P, TILES, E])
        top1 = sb("top1", [P, TILES])
        beats = sb("beats", [P, TILES, E, E])
        ties = sb("ties", [P, TILES, E, E])
        rank = sb("rank", [P, TILES, E])
        half_sel = sb("half_sel", [P, TILES, E])
        below = sb("below", [P, TILES, E])
        below_sel = sb("below_sel", [P, TILES, E])
        gap = sb("gap", [P, TILES])
        gate_arg = sb("gate_arg", [P, TILES, E])
        gate_tanh = sb("gate_tanh", [P, TILES, E])
        gate_w = sb("gate_w", [P, TILES, E])
        gate_hi = sb("gate_hi", [P, TILES, E], F32R)
        gate_split = sb("gate_split", [P, TILES, 2, E])
        gate_T = sb("gate_T", [2 * E, T], F32R)
        gate_bc = sb("gate_bc", [P, 2, E, T])
        weighted = sb("weighted", [P, TR, T])
        ident = sb("ident", [P, P])
        lower = sb("lower", [P, E, E])
        pick_f32 = sb("pick_f32", [2 * E, E, P])
        pick = sb("pick", [2 * E, E, P], F32R)
        bn = sb("bn", [P, NTILES, 6])
        mv = sb("mv", [P, NTILES, 2])
        var_eps = sb("var_eps", [P, NTILES])
        std = sb("std", [P, NTILES])
        rstd = sb("rstd", [P, NTILES])
        ema_in = sb("ema_in", [P, 4, N])
        ema_e = sb("ema_e", [P, 2, N])
        ema_s = sb("ema_s", [P, 2, N])
        ema_pa = sb("ema_pa", [P, N])
        ema_q = sb("ema_q", [P, N])
        ema_c = sb("ema_c", [P, 3, N])
        omega_half = sb("omega_half", [P, 1])
        q_tab = sb("q_tab", [P, N, T])
        zeros = sb("zeros", [P, T])
        ema = sb("ema", [P, N, 1 + CH])
        pre = sb("pre", [P, CH])
        pre_tanh = sb("pre_tanh", [P, CH])
        warm = sb("warm", [P, 1])

        z = ctx.enter_context(nc.psum_tensor("z", [P, ZR, T], F32))
        y = ctx.enter_context(nc.psum_tensor("y", [P, YR, T], F32))
        misc = ctx.enter_context(nc.psum_tensor("misc", [P, 2, T], F32))
        b1_col = cols[:, 0:E * FC]
        b2_col = cols[:, E * FC:E * FC + E]
        omega_col = cols[:, E * FC + E:ROWS]

        x_in = [sem(f"x_in{b}") for b in range(B)]
        w1_in = [sem(f"w1_in{e}") for e in range(E)]
        w2_in = [sem(f"w2_in{e}") for e in range(E)]
        rows_in = sem("rows_in")
        small_in = sem("small_in")
        out_done = sem("out_done")
        consts = sem("consts")
        pick_ready = sem("pick_ready")
        stats = sem("stats")
        std_ready = sem("std_ready")
        rstd_ready = sem("rstd_ready")
        xn_ready = sem("xn_ready")
        xnT_psum = sem("xnT_psum")
        xnT_ready = sem("xnT_ready")
        state_ready = sem("state_ready")
        cols_psum = sem("cols_psum")
        cols_ready = sem("cols_ready")
        w_hi = sem("w_hi")
        w_lo = sem("w_lo")
        wg_ready = sem("wg_ready")
        ema_exp = sem("ema_exp")
        ema_chain = sem("ema_chain")
        q_ready = sem("q_ready")
        z_full = sem("z_full")
        gelu_done = sem("gelu_done")
        hi_act = sem("hi_act")
        hi_dve = sem("hi_dve")
        lo_done = sem("lo_done")
        y_full = sem("y_full")
        combined = sem("combined")
        added = sem("added")
        cur_hi_ready = sem("cur_hi_ready")
        cur_ready = sem("cur_ready")
        lg_psum = sem("lg_psum")
        gate_step = sem("gate_step")
        gap_done = sem("gap_done")
        tanh_done = sem("tanh_done")
        gate_ready = sem("gate_ready")
        gateT_psum = sem("gateT_psum")
        gateT_ready = sem("gateT_ready")
        bc_psum = sem("bc_psum")
        bc_ready = sem("bc_ready")
        ema_step = sem("ema_step")
        pre_tanh_done = sem("pre_tanh_done")
        final_T = sem("final_T")
        final_psum = sem("final_psum")
        final_ready = sem("final_ready")

        GATE_STEPS = 12
        EMA_STEPS = 7

        def wait(eng, s, value):
            if not isinstance(value, int) or value > 0:
                eng.wait_ge(s, value)

        def block_of(k, parity):
            turn = (k - parity) // 2
            return 2 * (turn // R) + parity, turn % R

        def tokens(b, size=T):
            return bass.ds(b * size, size)

        def run_slots(eng, slot):
            slot(0, 0, first=True)
            with eng.Fori(0, SLOTS // 2 - 1) as i:
                slot(2 * i + 1, 1)
                slot(2 * i + 2, 0)
            slot(SLOTS - 1, 1, last=True)

        block = ctx.enter_context(nc.Block())

        @block.sync
        def _(sp):
            for b in range(B):
                sp.dma_start(x_tok[:, b * TILES:(b + 1) * TILES, :], x_v[b]).then_inc(x_in[b], 16)
            for e in range(E):
                sp.dma_start(w2_raw[:, e], W2[e].rearrange("(c p) h -> p c h", p=P)).then_inc(w2_in[e], 16)
            for b in range(B):
                sp.wait_ge(final_ready, b + 1)
                sp.dma_start(out_v[b], x_tok[:, b * TILES:(b + 1) * TILES, :]).then_inc(out_done, 16)
            sp.wait_ge(out_done, 16 * B)

        @block.gpsimd
        def _(pool):
            start_reg = pool.alloc_register("start_reg")
            pool.memset(ident[:], 0.0).then_inc(consts, 1)
            pool.wait_ge(consts, 1)
            pool.affine_select(out=ident[:], in_=ident[:], compare_op=ALU.not_equal, fill=1.0, base=0,
                               pattern=[[-1, P]], channel_multiplier=1).then_inc(consts, 1)
            pool.memset(lower[:], 0.0).then_inc(consts, 1)
            pool.wait_ge(consts, 3)
            pool.affine_select(out=lower[:], in_=lower[:], compare_op=ALU.is_ge, fill=1.0, base=0,
                               pattern=[[-1, E], [1, E]], channel_multiplier=0).then_inc(consts, 1)
            pool.memset(pick_f32[:], 0.0).then_inc(consts, 1)
            pool.wait_ge(consts, 5)
            pool.affine_select(out=pick_f32[:], in_=pick_f32[:], compare_op=ALU.not_equal, fill=1.0, base=0,
                               pattern=[[-1, E], [0, P]], channel_multiplier=1).then_inc(consts, 1)
            pool.wait_ge(consts, 6)
            pool.affine_select(out=pick_f32[:], in_=pick_f32[:], compare_op=ALU.not_equal, fill=1.0, base=-E,
                               pattern=[[-1, E], [0, P]], channel_multiplier=1).then_inc(consts, 1)
            pool.memset(zeros[:], 0.0).then_inc(consts, 1)

            def tokens_after_wait(b):
                if isinstance(b, int):
                    return tokens(b)
                pool.reg_mov(start_reg, b * T)
                return bass.ds(pool.snap(start_reg, min_val=0, max_val=(B - 1) * T), T)

            def split_state(k, b, parity):
                pool.wait_ge(cur_hi_ready, k + 1)
                at = tokens_after_wait(b)
                pool.tensor_tensor(cur_lo[:, parity, :], state[:, at],
                                   cur_hi[:, parity, :].bitcast(F32), ALU.subtract).then_inc(cur_ready, 1)

            for b in range(B):
                pool.wait_ge(xnT_ready, b + 1)
                pool.tensor_copy(state[:, tokens(b)], xn_T[:, tokens(b)]).then_inc(state_ready, 1)
                if b == 0:
                    split_state(0, 0, 0)
            for e in range(E):
                pool.wait_ge(w_hi, 2 * e + 1)
                pool.tensor_tensor(w1_lo[:, e], w1_raw[:, e], w1_hi[:, e].bitcast(F32),
                                   ALU.subtract).then_inc(w_lo, 1)
                pool.wait_ge(w_hi, 2 * e + 2)
                pool.tensor_tensor(w2_lo[:, e], w2_raw[:, e], w2_hi[:, e].bitcast(F32),
                                   ALU.subtract).then_inc(w_lo, 1)
            pool.wait_ge(q_ready, 1)
            pool.wait_ge(consts, 8)
            for n in range(N):
                pool.tensor_scalar(q_tab[:, n, :], zeros[:], ema_q[:, n:n + 1], None, ALU.add).then_inc(consts, 1)
            pool.wait_ge(consts, 8 + N)
            pool.memset(q_tab[:, :, 0:1], 0.0).then_inc(q_ready, 1)

            def slot(k, parity, first=False, last=False):
                b, _ = block_of(k, parity)
                if not first:
                    prev, _ = block_of(k - 1, 1 - parity)
                    pool.wait_ge(combined, E * k)
                    pool.wait_ge(added, E * k - 1)
                    at = tokens_after_wait(prev)
                    pool.tensor_tensor(state[:, at], state[:, at], weighted[:, E - 1, :],
                                       ALU.add).then_inc(added, 1)
                if not last:
                    nxt, _ = block_of(k + 1, 1 - parity)
                    split_state(k + 1, nxt, 1 - parity)
                for e in range(E - 1):
                    pool.wait_ge(combined, E * k + e + 1)
                    wait(pool, added, E * k + e)
                    at = tokens_after_wait(b)
                    pool.tensor_tensor(state[:, at], state[:, at], weighted[:, e, :],
                                       ALU.add).then_inc(added, 1)

            run_slots(pool, slot)
            pool.wait_ge(combined, E * SLOTS)
            pool.wait_ge(added, E * SLOTS - 1)
            pool.tensor_tensor(state[:, tokens(B - 1)], state[:, tokens(B - 1)], weighted[:, E - 1, :],
                               ALU.add).then_inc(added, 1)

        @block.scalar
        def _(act):
            for b, v in enumerate((delta, alpha)):
                act.dma_start(ema_in[:, b, :], v.rearrange("d n o -> d (n o)")).then_inc(small_in, 16)
            act.dma_start(w1_raw[:, 0], W1[0]).then_inc(w1_in[0], 16)
            act.dma_start(rows[0:E * FC, :], b1.rearrange("e (c p) -> (e c) p", p=P)).then_inc(rows_in, 16)
            act.dma_start(rows[E * FC:E * FC + E, :], b2).then_inc(rows_in, 16)
            act.dma_start(rows[E * FC + E:ROWS, :], omega.rearrange("(o p) -> o p", o=1)).then_inc(rows_in, 16)
            act.dma_start(wg_raw[:], Wg.rearrange("r h e -> h r e")).then_inc(small_in, 16)
            act.dma_start(bg_bc[:].rearrange("p r e -> p (r e)"),
                          bg.rearrange("r e -> (r e)").partition_broadcast(P)).then_inc(small_in, 16)
            act.dma_start(ema_in[:, 2, :], beta.rearrange("d n o -> d (n o)")).then_inc(small_in, 16)
            act.dma_start(ema_in[:, 3, :], gamma).then_inc(small_in, 16)
            for e in range(1, E):
                act.dma_start(w1_raw[:, e], W1[e]).then_inc(w1_in[e], 16)
            act.wait_ge(small_in, 16 * 6)
            nc.scalar.activation(ema_e[:], ema_in[:, 0:2, :], ACT.Exp, scale=-1.0).then_inc(ema_exp, 1)
            for b in range(B):
                act.wait_ge(stats, 3 * b + 3)
                nc.scalar.activation(std[:, b * TILES:(b + 1) * TILES], var_eps[:, b * TILES:(b + 1) * TILES],
                                     ACT.Sqrt).then_inc(std_ready, 1)
            act.wait_ge(consts, 2)
            nc.scalar.activation(warm[:], ident[:, 0:1], ACT.Gelu_apprx_tanh)

            act.wait_ge(cols_psum, 1)
            nc.scalar.copy(cols[:], misc[:, 1, 0:ROWS]).then_inc(cols_ready, 1)
            for b in range(B):
                act.wait_ge(xnT_psum, b + 1)
                nc.scalar.copy(xn_T[:, tokens(b)], misc[:, 0, :] if b % 2 == 0 else y[:, 0, :]).then_inc(xnT_ready, 1)
                if b == 0:
                    for e in range(E):
                        act.wait_ge(w1_in[e], 16)
                        nc.scalar.copy(w1_hi[:, e], w1_raw[:, e]).then_inc(w_hi, 1)
                        act.wait_ge(w2_in[e], 16)
                        nc.scalar.copy(w2_hi[:, e], w2_raw[:, e]).then_inc(w_hi, 1)
            act.wait_ge(consts, 7)
            nc.scalar.copy(pick[:], pick_f32[:]).then_inc(pick_ready, 1)

            def gate_tanh_of(k):
                act.wait_ge(gate_step, GATE_STEPS * (k + 1))
                nc.scalar.activation(gate_tanh[:], gate_arg[:], ACT.Tanh).then_inc(tanh_done, 1)

            def gate_T_copy(k):
                act.wait_ge(gateT_psum, k + 1)
                wait(act, bc_psum, E * k)
                nc.scalar.copy(gate_T[:], misc[0:2 * E, 1, :]).then_inc(gateT_ready, 1)

            gate_tanh_of(0)

            def slot(k, parity, first=False, last=False):
                for j in range(0, STEPS, 2):
                    for i in (j, j + 1):
                        act.wait_ge(z_full, STEPS * k + i + 1)
                        nc.scalar.activation(z[:, i % ZR, :], z[:, i % ZR, :], ACT.Gelu_apprx_tanh,
                                             bias=b1_col[:, i:i + 1]).then_inc(gelu_done, 1)
                    for i in (j, j + 1):
                        if i in HI_ON_ACT:
                            act.wait_ge(gelu_done, STEPS * k + i + 1)
                            nc.scalar.copy(h_hi[:, i % ZR, :], z[:, i % ZR, :]).then_inc(hi_act, 1)
                    if j == 0:
                        gate_T_copy(k)
                    if j % FC == 2:
                        e = j // FC
                        act.wait_ge(bc_psum, E * k + e + 1)
                        nc.scalar.copy(gate_bc[:, parity, e, :], misc[:, 0, :]).then_inc(bc_ready, 1)
                    if j == 10 and parity == 1:
                        c = (k - 1) // 2
                        act.wait_ge(ema_step, EMA_STEPS * (c + 1))
                        nc.scalar.activation(pre_tanh[:], pre[:], ACT.Tanh).then_inc(pre_tanh_done, 1)
                    if j == 12 and not last:
                        gate_tanh_of(k + 1)

            run_slots(act, slot)

        @block.vector
        def _(dve):
            def ln_stats(b):
                t0 = b * TILES
                dve.wait_ge(x_in[b], 16)
                for t in range(t0, t0 + TILES):
                    ins = dve.bn_stats(bn[:, t, :], x_tok[:, t, :])
                ins.then_inc(stats, 1)
                dve.wait_ge(stats, 3 * b + 1)
                for t in range(t0, t0 + TILES):
                    ins = dve.bn_aggr(mv[:, t, :], bn[:, t, :])
                ins.then_inc(stats, 1)
                dve.wait_ge(stats, 3 * b + 2)
                dve.tensor_scalar(var_eps[:, t0:t0 + TILES], mv[:, t0:t0 + TILES, 1], LN_EPS, None,
                                  ALU.add).then_inc(stats, 1)

            def ln_apply(b):
                t0 = b * TILES
                dve.wait_ge(std_ready, b + 1)
                dve.reciprocal(rstd[:, t0:t0 + TILES], std[:, t0:t0 + TILES]).then_inc(rstd_ready, 1)
                dve.wait_ge(rstd_ready, b + 1)
                for t in range(TILES):
                    ins = dve.tensor_scalar(xn_tok[:, b, t, :], x_tok[:, t0 + t, :], mv[:, t0 + t, 0:1],
                                            rstd[:, t0 + t:t0 + t + 1], ALU.subtract, ALU.mult)
                ins.then_inc(xn_ready, 1)

            ln_stats(0)
            ln_stats(1)
            ln_apply(0)
            for b in range(2, B):
                ln_stats(b)
                ln_apply(b - 1)
            ln_apply(B - 1)
            dve.wait_ge(small_in, 16 * 6)
            dve.tensor_copy(wg_split[:, :, 0, :], wg_raw[:]).then_inc(wg_ready, 1)
            dve.wait_ge(wg_ready, 1)
            dve.tensor_tensor(wg_split[:, :, 1, :], wg_raw[:], wg_split[:, :, 0, :].bitcast(F32),
                              ALU.subtract).then_inc(wg_ready, 1)
            dve.wait_ge(ema_exp, 1)
            dve.tensor_scalar(ema_s[:], ema_e[:], 1.0, None, ALU.add).then_inc(ema_chain, 1)
            dve.wait_ge(ema_chain, 1)
            dve.reciprocal(ema_e[:], ema_s[:]).then_inc(ema_chain, 1)
            dve.wait_ge(ema_chain, 2)
            dve.tensor_tensor(ema_pa[:], ema_e[:, 0, :], ema_e[:, 1, :], ALU.mult).then_inc(ema_chain, 1)
            dve.wait_ge(ema_chain, 3)
            dve.tensor_scalar(ema_q[:], ema_pa[:], -1.0, 1.0, ALU.mult, ALU.add).then_inc(q_ready, 1)
            dve.tensor_tensor(ema_c[:, 0, :], ema_e[:, 0, :], ema_in[:, 2, :], ALU.mult).then_inc(ema_chain, 1)
            dve.tensor_scalar(ema_c[:, 1, :], ema_in[:, 3, :], EMA_SCALE, 0.5, ALU.mult,
                              ALU.mult).then_inc(ema_chain, 1)
            dve.wait_ge(ema_chain, 5)
            dve.tensor_tensor(ema_c[:, 2, :], ema_c[:, 0, :], ema_c[:, 1, :], ALU.mult).then_inc(ema_chain, 1)
            dve.wait_ge(cols_ready, 1)
            dve.tensor_scalar(omega_half[:], omega_col, 0.5, None, ALU.mult).then_inc(ema_chain, 1)

            def gate_ops(k, rnd):
                g0 = GATE_STEPS * k

                def logits_a():
                    dve.wait_ge(lg_psum, k + 1)
                    bias = bg_bc[:, bass.ds(rnd, 1), :].broadcast_to([P, TILES, E])
                    dve.tensor_tensor(lg[:], lg_ps[:, :, 0, :], bias, ALU.add).then_inc(gate_step, 1)

                def logits_b():
                    dve.wait_ge(gate_step, g0 + 1)
                    dve.tensor_tensor(lg[:], lg_ps[:, :, 1, :], lg[:], ALU.add).then_inc(gate_step, 1)

                def top():
                    dve.wait_ge(gate_step, g0 + 2)
                    dve.tensor_reduce(top1[:], lg[:], AX_X, ALU.max).then_inc(gate_step, 1)

                def rank_beats():
                    other = lg[:].unsqueeze(2).broadcast_to([P, TILES, E, E])
                    mine = lg[:].unsqueeze(3).broadcast_to([P, TILES, E, E])
                    dve.tensor_tensor(beats[:], other, mine, ALU.is_gt).then_inc(gate_step, 1)

                def rank_ties():
                    other = lg[:].unsqueeze(2).broadcast_to([P, TILES, E, E])
                    mine = lg[:].unsqueeze(3).broadcast_to([P, TILES, E, E])
                    dve.tensor_tensor(ties[:], other, mine, ALU.is_equal).then_inc(gate_step, 1)

                def rank_low_ties():
                    dve.wait_ge(gate_step, g0 + 5)
                    dve.tensor_tensor(ties[:], ties[:], lower[:].unsqueeze(1).broadcast_to([P, TILES, E, E]),
                                      ALU.mult).then_inc(gate_step, 1)

                def rank_all():
                    dve.wait_ge(gate_step, g0 + 6)
                    dve.tensor_tensor(beats[:], beats[:], ties[:], ALU.add).then_inc(gate_step, 1)

                def ranks():
                    dve.wait_ge(gate_step, g0 + 7)
                    dve.tensor_reduce(rank[:], beats[:], AX_X, ALU.add).then_inc(gate_step, 1)

                def distance():
                    dve.tensor_tensor(below[:], lg[:], top1[:].unsqueeze(2).broadcast_to([P, TILES, E]),
                                      ALU.subtract).then_inc(gate_step, 1)

                def selected():
                    dve.wait_ge(gate_step, g0 + 9)
                    dve.tensor_scalar(half_sel[:], rank[:], 2.0, 0.5, ALU.is_lt, ALU.mult).then_inc(gate_step, 1)
                    dve.wait_ge(gate_step, g0 + 10)
                    dve.tensor_tensor(below_sel[:], below[:], half_sel[:], ALU.mult).then_inc(gate_step, 1)

                def softmax_arg():
                    dve.wait_ge(gate_step, g0 + 11)
                    dve.tensor_reduce(gap[:], below_sel[:], AX_X, ALU.add).then_inc(gap_done, 1)
                    dve.wait_ge(gap_done, k + 1)
                    dve.tensor_tensor(gate_arg[:], below[:], gap[:].unsqueeze(2).broadcast_to([P, TILES, E]),
                                      ALU.subtract).then_inc(gate_step, 1)

                return [[logits_a, logits_b], [top, rank_beats, rank_ties], [rank_low_ties, rank_all], [ranks, distance],
                        [selected, softmax_arg]]

            def gate_weights(k):
                dve.wait_ge(tanh_done, k + 1)
                dve.scalar_tensor_tensor(out=gate_w[:], in0=gate_tanh[:], scalar=1.0, in1=half_sel[:],
                                         op0=ALU.add, op1=ALU.mult).then_inc(gate_ready, 1)
                dve.wait_ge(gate_ready, 4 * k + 1)
                dve.tensor_copy(gate_hi[:], gate_w[:]).then_inc(gate_ready, 1)
                dve.wait_ge(gate_ready, 4 * k + 2)
                dve.tensor_copy(gate_split[:, :, 0, :], gate_hi[:].bitcast(F32)).then_inc(gate_ready, 1)
                dve.tensor_tensor(gate_split[:, :, 1, :], gate_w[:], gate_hi[:].bitcast(F32),
                                  ALU.subtract).then_inc(gate_ready, 1)

            lg_ps = misc[:, 1, 0:TILES * 2 * E].rearrange("p (t s e) -> p t s e", t=TILES, s=2)
            dve.wait_ge(state_ready, 1)
            dve.tensor_copy(cur_hi[:, 0, :], state[:, tokens(0)]).then_inc(cur_hi_ready, 1)
            for ops in gate_ops(0, 0):
                for op in ops:
                    op()
            gate_weights(0)

            def split_state_hi(k, b, parity):
                dve.tensor_copy(cur_hi[:, parity, :], state[:, tokens(b)]).then_inc(cur_hi_ready, 1)

            def combine(k, e, parity):
                dve.wait_ge(y_full, E * k + e + 1)
                dve.wait_ge(bc_ready, E * k + e + 1)
                if e < E - 1 or isinstance(k, int):
                    wait(dve, added, E * k + e + 1 - TR)
                dve.scalar_tensor_tensor(out=weighted[:, e, :], in0=y[:, e % YR, :], scalar=b2_col[:, e:e + 1],
                                         in1=gate_bc[:, parity, e, :], op0=ALU.add,
                                         op1=ALU.mult).then_inc(combined, 1)

            dve.memset(ema[:, :, 0:1], 0.0).then_inc(ema_step, 1)

            def attention(c):
                s0 = EMA_STEPS * c + 1
                chunk = tokens(c, CH)
                half = tokens(c % HALVES, CH)

                def scan(n):
                    def op():
                        dve.wait_ge(q_ready, 2)
                        dve.wait_ge(ema_step, s0)
                        dve.tensor_tensor_scan(ema[:, n, 1:1 + CH], q_tab[:, n, half], xn_T[:, chunk],
                                               ema[:, n, 0:1], ALU.mult, ALU.add).then_inc(ema_step, 1)
                    return op

                def residual():
                    dve.tensor_scalar(pre[:], xn_T[:, chunk], omega_half[:], None, ALU.mult).then_inc(ema_step, 1)

                def carry():
                    dve.wait_ge(ema_step, s0 + 2)
                    dve.tensor_copy(ema[:, :, 0:1], ema[:, :, CH:CH + 1]).then_inc(ema_step, 1)

                def mix(n):
                    def op():
                        dve.wait_ge(ema_step, s0 + 4 + n)
                        dve.scalar_tensor_tensor(out=pre[:], in0=ema[:, n, 1:1 + CH], scalar=ema_c[:, 2, n:n + 1],
                                                 in1=pre[:], op0=ALU.mult, op1=ALU.add).then_inc(ema_step, 1)
                    return op

                def silu():
                    dve.wait_ge(pre_tanh_done, c + 1)
                    dve.scalar_tensor_tensor(out=attn_T[:, chunk], in0=pre_tanh[:], scalar=1.0, in1=pre[:],
                                             op0=ALU.add, op1=ALU.mult).then_inc(ema_step, 1)

                return [[scan(0)], [scan(1)], [residual, carry], [mix(0)], [mix(1)], [silu]]

            def slot(k, parity, first=False, last=False):
                extra = {}
                if not last:
                    nxt, rnd = block_of(k + 1, 1 - parity)

                    def next_state():
                        if first:
                            dve.wait_ge(state_ready, 2)
                        else:
                            dve.wait_ge(added, E * k)
                            dve.wait_ge(z_full, STEPS * k)
                        split_state_hi(k + 1, nxt, 1 - parity)

                    extra[3] = [next_state]
                    for n, ops in enumerate(gate_ops(k + 1, rnd)):
                        extra.setdefault(6 + n, []).extend(ops)
                    extra[13] = [lambda: gate_weights(k + 1)]
                if parity == 1:
                    for j, ops in zip((0, 2, 3, 5, 8, 14), attention((k - 1) // 2)):
                        extra.setdefault(j, []).extend(ops)
                for j in range(STEPS):
                    if j in HI_ON_DVE:
                        dve.wait_ge(gelu_done, STEPS * k + j + 1)
                        dve.tensor_copy(h_hi[:, j % ZR, :], z[:, j % ZR, :]).then_inc(hi_dve, 1)
                        n = HI_ON_DVE.index(j)
                        dve.wait_ge(hi_dve, len(HI_ON_DVE) * k + n + 1)
                    else:
                        dve.wait_ge(hi_act, len(HI_ON_ACT) * k + HI_ON_ACT.index(j) + 1)
                    dve.tensor_tensor(h_lo[:, j % ZR, :], z[:, j % ZR, :], h_hi[:, j % ZR, :].bitcast(F32),
                                      ALU.subtract).then_inc(lo_done, 1)
                    if j == 1 and not first:
                        combine(k - 1, E - 1, 1 - parity)
                    if j % FC == 2 and j > FC:
                        combine(k, j // FC - 1, parity)
                    for op in extra.get(j, []):
                        op()

            def final_add(b):
                dve.wait_ge(final_psum, b + 1)
                xs = x_tok[:, b * TILES:(b + 1) * TILES, :].rearrange("p t h -> p (t h)")
                dve.tensor_tensor(xs, z[:, b % ZR, :], xs, ALU.add).then_inc(final_ready, 1)

            run_slots(dve, slot)
            combine(SLOTS - 1, E - 1, 1)
            for b in range(B):
                if b >= B - 2:
                    dve.wait_ge(added, E * (SLOTS - (B - 1 - b)))
                dve.wait_ge(ema_step, EMA_STEPS * SLOTS // 2 + 1)
                dve.tensor_tensor(state[:, tokens(b)], state[:, tokens(b)], attn_T[:, tokens(b)],
                                  ALU.add).then_inc(final_T, 1)
                if b >= 1:
                    final_add(b - 1)
            final_add(B - 1)

        @block.tensor
        def _(pe):
            pe.wait_ge(consts, 2)
            pe.wait_ge(rows_in, 48)
            pe.transpose(misc[:, 1, 0:ROWS], rows[:], ident[0:ROWS, 0:ROWS]).then_inc(cols_psum, 1)
            for b in range(B):
                pe.wait_ge(xn_ready, b + 1)
                if b >= 2:
                    pe.wait_ge(xnT_ready, b - 1)
                bank = misc[:, 0, :] if b % 2 == 0 else y[:, 0, :]
                for t in range(TILES):
                    ins = pe.transpose(bank[:, t * P:(t + 1) * P], xn_tok[:, b, t, :], ident[:])
                ins.then_inc(xnT_psum, 1)

            def logits(k, rnd, parity):
                pe.wait_ge(cur_ready, k + 1)
                if isinstance(k, int) and k == 0:
                    pe.wait_ge(wg_ready, 2)
                    pe.wait_ge(cols_ready, 1)
                else:
                    pe.wait_ge(gateT_ready, k)
                for t in range(TILES):
                    w = wg_split[:, bass.ds(rnd, 1), :, :].rearrange("p r s e -> p (r s e)")
                    dst = misc[:, 1, t * 2 * E:(t + 1) * 2 * E]
                    pe.matmul(dst, cur_hi[:, parity, t * P:(t + 1) * P], w, start=True, stop=False)
                    ins = pe.matmul(dst, cur_lo[:, parity, t * P:(t + 1) * P], w, start=False, stop=True)
                ins.then_inc(lg_psum, 1)

            def gate_transpose(k):
                pe.wait_ge(gate_ready, 4 * (k + 1))
                for t in range(TILES):
                    ins = pe.transpose(misc[0:2 * E, 1, t * P:(t + 1) * P],
                                       gate_split[:, t, :, :].rearrange("p s e -> p (s e)"), ident[:])
                ins.then_inc(gateT_psum, 1)

            def broadcast(k, e):
                if e == 0:
                    pe.wait_ge(gateT_ready, k + 1)
                wait(pe, bc_ready, E * k + e)
                pe.matmul(misc[:, 0, :], pick[:, e, :], gate_T[:], start=True, stop=True).then_inc(bc_psum, 1)

            def up(j, parity):
                e, c = divmod(j, FC)
                hi, lo = (w[:, e, c * P:(c + 1) * P] for w in (w1_hi, w1_lo))
                dst = z[:, j % ZR, :]
                pe.matmul(dst, hi, cur_hi[:, parity, :], start=True, stop=False)
                pe.matmul(dst, hi, cur_lo[:, parity, :], start=False, stop=False)
                pe.matmul(dst, lo, cur_hi[:, parity, :], start=False, stop=True).then_inc(z_full, 1)

            def down(k, j):
                e, c = divmod(j, FC)
                pe.wait_ge(lo_done, STEPS * k + j + 1)
                if c == 0:
                    wait(pe, combined, E * k + e + 1 - YR)
                hi, lo = (w[:, e, c, :] for w in (w2_hi, w2_lo))
                dst = y[:, e % YR, :]
                pe.matmul(dst, hi, h_hi[:, j % ZR, :], start=(c == 0), stop=False)
                pe.matmul(dst, hi, h_lo[:, j % ZR, :], start=False, stop=False)
                ins = pe.matmul(dst, lo, h_hi[:, j % ZR, :], start=False, stop=(c == FC - 1))
                if c == FC - 1:
                    ins.then_inc(y_full, 1)

            logits(0, 0, 0)
            gate_transpose(0)
            pe.wait_ge(pick_ready, 1)
            pe.wait_ge(xnT_ready, B)
            pe.wait_ge(w_lo, 2 * E)
            for j in range(LAG):
                up(j, 0)

            def slot(k, parity, first=False, last=False):
                for j in range(STEPS):
                    if j + LAG < STEPS:
                        up(j + LAG, parity)
                    elif not last:
                        up(j + LAG - STEPS, 1 - parity)
                    down(k, j)
                    if j in BROADCAST_AT:
                        broadcast(k, BROADCAST_AT.index(j))
                    if j == 5 and not last:
                        logits(k + 1, block_of(k + 1, 1 - parity)[1], 1 - parity)
                    if j == 14 and not last:
                        gate_transpose(k + 1)

            run_slots(pe, slot)
            for b in range(B):
                pe.wait_ge(final_T, b + 1)
                if b >= ZR:
                    pe.wait_ge(final_ready, b - ZR + 1)
                for t in range(TILES):
                    ins = pe.transpose(z[:, b % ZR, t * P:(t + 1) * P],
                                       state[:, b * T + t * P:b * T + (t + 1) * P], ident[:])
                ins.then_inc(final_psum, 1)


_INS = ['L0_attn_x', 'L0_attn_delta', 'L0_attn_alpha', 'L0_attn_beta', 'L0_attn_gamma', 'L0_attn_omega',
        'L0_ffn_Wg', 'L0_ffn_bg', 'L0_ffn_W1', 'L0_ffn_b1', 'L0_ffn_W2', 'L0_ffn_b2']
_OUTS = [((8, 512, 128), 'float32')]


def kernel(**inputs):
    import numpy as _np
    import concourse.bacc as _bacc
    from concourse import mybir as _mybir
    from concourse.bass_utils import run_bass_kernel_spmd as _run

    nc = _bacc.Bacc("TRN2", target_bir_lowering=False, num_devices=1)
    arrays, args = {}, []
    for name in _INS:
        a = _np.ascontiguousarray(inputs[name])
        arrays[f"in_{name}_dram"] = a
        args.append(nc.dram_tensor(f"in_{name}_dram", a.shape, _mybir.dt.from_np(a.dtype), kind="ExternalInput").ap())
    for i, (shape, dtype) in enumerate(_OUTS):
        dt = _mybir.dt.from_np(_np.dtype(dtype))
        args.append(nc.dram_tensor(f"out_{i}_dram", shape, dt, kind="ExternalOutput").ap())
    ema_and_routed_ffn_kernel(nc, *args)
    r = _run(nc, [arrays], core_ids=[0])
    got = tuple(r.results[0][f"out_{i}_dram"] for i in range(len(_OUTS)))
    return got[0]
```

```python
from contextlib import ExitStack

import concourse.bass as bass
from concourse import mybir

F32 = mybir.dt.float32
F32R = mybir.dt.float32r
I32 = mybir.dt.int32
ALU = mybir.AluOpType
ACT = mybir.ActivationFunctionType
AX_X = mybir.AxisListType.X


def ema_and_routed_ffn_kernel(nc, x, delta, alpha, beta, gamma, omega, Wg, bg, W1, b1, W2, b2, out):
    B, T, H = x.shape
    R, _, E = Wg.shape
    F = W1.shape[2]
    N = delta.shape[1]
    P = 128
    FC = F // P
    STEPS = E * FC
    TILES = T // P
    NTILES = B * TILES
    PAIRS = B // 2
    SLOTS = B * R
    LAG = 3
    ZR = 4
    YR = 2
    TR = 4
    CH = B * T // (SLOTS // 2)
    HALVES = T // CH
    LN_EPS = 1e-05
    RSQRT_MAGIC = 0x5F3759DF
    NEWTON = 3
    EARLY = 2
    PER_SLOT = 2
    INTAKE_SLOTS = (B - EARLY) * TILES // PER_SLOT
    EMA_SCALE = (1.0 / N) ** 0.5
    ROWS = E * FC + E + 1
    assert INTAKE_SLOTS % 2 == 0 and EARLY == 2
    assert H == P and T == 512 and SLOTS % 2 == 0 and HALVES == 2 and STEPS == 16
    HI_ON_DVE = (4,12,15)
    GATE_T_AT = 13
    TANH_AT = 12
    HI_ON_ACT = [j for j in range(STEPS) if j not in HI_ON_DVE]

    x_v = x.rearrange("b (t p) h -> b p t h", p=P)
    out_v = out.rearrange("b (t p) h -> b p t h", p=P)

    with ExitStack() as ctx:
        def sb(name, shape, dt=F32):
            return ctx.enter_context(nc.sbuf_tensor(name, shape, dt))

        def sem(name):
            return ctx.enter_context(nc.semaphore(name))

        x_tok = sb("x_tok", [P, NTILES, H])
        xn_early = sb("xn_early", [P, EARLY, TILES, H])
        xn_pair = sb("xn_pair", [P, PER_SLOT, H])
        xn_T = sb("xn_T", [P, B * T])
        state = sb("state", [P, B * T])
        attn_T = sb("attn_T", [P, B * T])
        w1_raw = sb("w1_raw", [P, E, F])
        w2_raw = sb("w2_raw", [P, E, FC, H])
        w1_hi = sb("w1_hi", [P, E, F], F32R)
        w1_lo = sb("w1_lo", [P, E, F], F32R)
        w2_hi = sb("w2_hi", [P, E, FC, H], F32R)
        w2_lo = sb("w2_lo", [P, E, FC, H], F32R)
        wg_raw = sb("wg_raw", [P, R, E])
        wg_split = sb("wg_split", [P, R, 2, E], F32R)
        bg_bc = sb("bg_bc", [P, R, E])
        rows = sb("rows", [ROWS, P])
        cols = sb("cols", [P, ROWS])
        cur_hi = sb("cur_hi", [P, 2, T], F32R)
        cur_lo = sb("cur_lo", [P, 2, T], F32R)
        h_hi = sb("h_hi", [P, ZR, T], F32R)
        h_lo = sb("h_lo", [P, ZR, T], F32R)
        lg = sb("lg", [P, TILES, E])
        top1 = sb("top1", [P, TILES])
        beats = sb("beats", [P, TILES, E, E])
        ties = sb("ties", [P, TILES, E, E])
        rank = sb("rank", [P, TILES, E])
        half_sel = sb("half_sel", [P, TILES, E])
        below = sb("below", [P, TILES, E])
        below_sel = sb("below_sel", [P, TILES, E])
        gap = sb("gap", [P, TILES])
        gate_arg = sb("gate_arg", [P, TILES, E])
        gate_tanh = sb("gate_tanh", [P, TILES, E])
        gate_w = sb("gate_w", [P, E, TILES])
        gate_T = sb("gate_T", [E * TILES, P])
        gate_rows = nc.dram_tensor("gate_rows", [E, T], F32, kind="Internal").ap()
        gate_bc = sb("gate_bc", [P, 2, E, T])
        weighted = sb("weighted", [P, TR, T])
        ident = sb("ident", [P, P])
        lower = sb("lower", [P, E, E])
        bn = sb("bn", [P, NTILES, 6])
        mv = sb("mv", [P, NTILES, 2])
        var_eps = sb("var_eps", [P, NTILES])
        half_bits = sb("half_bits", [P, NTILES], I32)
        newton = sb("newton", [P, NTILES])
        rstd = sb("rstd", [P, NTILES])
        ema_in = sb("ema_in", [P, 4, N])
        ema_e = sb("ema_e", [P, 2, N])
        ema_s = sb("ema_s", [P, 2, N])
        ema_pa = sb("ema_pa", [P, N])
        ema_q = sb("ema_q", [P, N])
        ema_c = sb("ema_c", [P, 3, N])
        omega_half = sb("omega_half", [P, 1])
        q_tab = sb("q_tab", [P, N, T])
        zeros = sb("zeros", [P, T])
        ema = sb("ema", [P, N, 1 + CH])
        pre = sb("pre", [P, CH])
        pre_tanh = sb("pre_tanh", [P, CH])
        warm = sb("warm", [P, 1])

        z = ctx.enter_context(nc.psum_tensor("z", [P, ZR, T], F32))
        y = ctx.enter_context(nc.psum_tensor("y", [P, YR, T], F32))
        misc = ctx.enter_context(nc.psum_tensor("misc", [P, 2, T], F32))
        b1_col = cols[:, 0:E * FC]
        b2_col = cols[:, E * FC:E * FC + E]
        omega_col = cols[:, E * FC + E:ROWS]

        x_in = [sem(f"x_in{b}") for b in range(EARLY + 1)]
        w1_in = [sem(f"w1_in{e}") for e in range(E)]
        w2_in = [sem(f"w2_in{e}") for e in range(E)]
        rows_in = sem("rows_in")
        gate_in = sem("gate_in")
        ema_coef_in = sem("ema_coef_in")
        out_done = sem("out_done")
        consts = sem("consts")
        stats = sem("stats")
        rstd_step = sem("rstd_step")
        xn_ready = sem("xn_ready")
        intake_xn = sem("intake_xn")
        intake_psum = sem("intake_psum")
        intake_T = sem("intake_T")
        intake_state = sem("intake_state")
        xnT_psum = sem("xnT_psum")
        xnT_ready = sem("xnT_ready")
        state_ready = sem("state_ready")
        cols_psum = sem("cols_psum")
        cols_ready = sem("cols_ready")
        w_hi = sem("w_hi")
        w_lo = sem("w_lo")
        wg_ready = sem("wg_ready")
        ema_exp = sem("ema_exp")
        ema_chain = sem("ema_chain")
        q_ready = sem("q_ready")
        z_full = sem("z_full")
        gelu_done = sem("gelu_done")
        hi_act = sem("hi_act")
        hi_dve = sem("hi_dve")
        lo_done = sem("lo_done")
        y_full = sem("y_full")
        combined = sem("combined")
        added = sem("added")
        cur_hi_ready = sem("cur_hi_ready")
        cur_ready = sem("cur_ready")
        lg_psum = sem("lg_psum")
        gate_step = sem("gate_step")
        gap_done = sem("gap_done")
        tanh_done = sem("tanh_done")
        gate_ready = sem("gate_ready")
        gateT_psum = sem("gateT_psum")
        gateT_ready = sem("gateT_ready")
        rows_out = sem("rows_out")
        bc_in = [sem(f"bc_in{e}") for e in range(E)]
        ema_step = sem("ema_step")
        pre_tanh_done = sem("pre_tanh_done")
        final_T = sem("final_T")
        final_psum = sem("final_psum")
        final_ready = sem("final_ready")

        GATE_STEPS = 12
        EMA_STEPS = 7

        def wait(eng, s, value):
            if not isinstance(value, int) or value > 0:
                eng.wait_ge(s, value)

        def block_of(k, parity):
            turn = (k - parity) // 2
            return 2 * (turn // R) + parity, turn % R

        def tokens(b, size=T):
            return bass.ds(b * size, size)

        def intake_tokens(k):
            return bass.ds((EARLY * TILES + PER_SLOT * (k - 1)) * P, PER_SLOT * P)

        def run_slots(eng, slot):
            slot(0, 0, first=True)
            with eng.Fori(0, INTAKE_SLOTS // 2) as i:
                slot(2 * i + 1, 1, intake=True)
                slot(2 * i + 2, 0, intake=True)
            with eng.Fori(INTAKE_SLOTS // 2, SLOTS // 2 - 1) as i:
                slot(2 * i + 1, 1)
                slot(2 * i + 2, 0)
            slot(SLOTS - 1, 1, last=True)

        block = ctx.enter_context(nc.Block())

        @block.sync
        def _(sp):
            def load_x(b):
                sp.dma_start(x_tok[:, b * TILES:(b + 1) * TILES, :], x_v[b]).then_inc(x_in[b], 16)

            def load_w2(e):
                sp.dma_start(w2_raw[:, e], W2[e].rearrange("(c p) h -> p c h", p=P)).then_inc(w2_in[e], 16)

            load_x(0)
            load_w2(0)
            load_x(1)
            for e in range(1, E):
                sp.dma_start(w1_raw[:, e], W1[e]).then_inc(w1_in[e], 16)
                load_w2(e)
            sp.dma_start(x_tok[:, EARLY * TILES:NTILES, :].rearrange("p (b t) h -> p b t h", t=TILES),
                         x[EARLY:B].rearrange("b (t p) h -> p b t h", p=P)).then_inc(x_in[EARLY], 16)

            count_regs = [sp.alloc_register(f"count{n}") for n in range(4)]

            def broadcast_gate(k, parity):
                counts = (k + 1, 16 * k, E * (k - 1), 16 * (k + 1))
                if not isinstance(k, int):
                    for register, count in zip(count_regs, counts):
                        sp.reg_mov(register, count)
                    counts = [sp.snap(register) for register in count_regs]
                transposed, last_in, used, in_dram = counts
                sp.wait_ge(gateT_ready, transposed)
                if not isinstance(k, int) or k > 0:
                    for e in range(E):
                        sp.wait_ge(bc_in[e], last_in)
                sp.dma_start(gate_rows.rearrange("e (t p) -> (e t) p", p=P), gate_T[:]).then_inc(rows_out, 16)
                if not isinstance(k, int) or k > 1:
                    sp.wait_ge(combined, used)
                sp.wait_ge(rows_out, in_dram)
                for e in range(E):
                    sp.dma_start(gate_bc[:, parity, e, :],
                                 gate_rows[e].partition_broadcast(P)).then_inc(bc_in[e], 16)

            broadcast_gate(0, 0)
            broadcast_gate(1, 1)
            with sp.Fori(1, SLOTS // 2) as i:
                broadcast_gate(2 * i, 0)
                broadcast_gate(2 * i + 1, 1)
            for b in range(B):
                sp.wait_ge(final_ready, b + 1)
                sp.dma_start(out_v[b], x_tok[:, b * TILES:(b + 1) * TILES, :]).then_inc(out_done, 16)
            sp.wait_ge(out_done, 16 * B)

        @block.gpsimd
        def _(pool):
            start_reg = pool.alloc_register("start_reg")
            pool.memset(ident[:], 0.0).then_inc(consts, 1)
            pool.wait_ge(consts, 1)
            pool.affine_select(out=ident[:], in_=ident[:], compare_op=ALU.not_equal, fill=1.0, base=0,
                               pattern=[[-1, P]], channel_multiplier=1).then_inc(consts, 1)
            pool.memset(lower[:], 0.0).then_inc(consts, 1)
            pool.wait_ge(consts, 3)
            pool.affine_select(out=lower[:], in_=lower[:], compare_op=ALU.is_ge, fill=1.0, base=0,
                               pattern=[[-1, E], [1, E]], channel_multiplier=0).then_inc(consts, 1)
            pool.memset(zeros[:], 0.0).then_inc(consts, 1)

            def tokens_after_wait(b):
                if isinstance(b, int):
                    return tokens(b)
                pool.reg_mov(start_reg, b * T)
                return bass.ds(pool.snap(start_reg, min_val=0, max_val=(B - 1) * T), T)

            def split_state(k, b, parity):
                pool.wait_ge(cur_hi_ready, k + 1)
                at = tokens_after_wait(b)
                pool.tensor_tensor(cur_lo[:, parity, :], state[:, at],
                                   cur_hi[:, parity, :].bitcast(F32), ALU.subtract).then_inc(cur_ready, 1)

            for e in range(E):
                pool.wait_ge(w_hi, 2 * e + 1)
                pool.tensor_tensor(w1_lo[:, e], w1_raw[:, e], w1_hi[:, e].bitcast(F32),
                                   ALU.subtract).then_inc(w_lo, 1)
                pool.wait_ge(w_hi, 2 * e + 2)
                pool.tensor_tensor(w2_lo[:, e], w2_raw[:, e], w2_hi[:, e].bitcast(F32),
                                   ALU.subtract).then_inc(w_lo, 1)
            def scan_multiplier():
                pool.wait_ge(consts, 5)
                pool.wait_ge(q_ready, 1)
                for n in range(N):
                    pool.tensor_scalar(q_tab[:, n, :], zeros[:], ema_q[:, n:n + 1], None, ALU.add).then_inc(consts, 1)
                pool.wait_ge(consts, 5 + N)
                pool.memset(q_tab[:, :, 0:1], 0.0).then_inc(q_ready, 1)

            def slot(k, parity, first=False, last=False, intake=False):
                b, _ = block_of(k, parity)
                if not first:
                    prev, _ = block_of(k - 1, 1 - parity)
                    pool.wait_ge(combined, E * k)
                    pool.wait_ge(added, E * k - 1)
                    at = tokens_after_wait(prev)
                    pool.tensor_tensor(state[:, at], state[:, at], weighted[:, E - 1, :],
                                       ALU.add).then_inc(added, 1)
                if not last:
                    nxt, _ = block_of(k + 1, 1 - parity)
                    split_state(k + 1, nxt, 1 - parity)
                if first:
                    scan_multiplier()
                for e in range(E - 1):
                    if e == 2 and intake:
                        pool.wait_ge(intake_T, k)
                        pool.reg_mov(start_reg, (EARLY * TILES + PER_SLOT * (k - 1)) * P)
                        at = bass.ds(pool.snap(start_reg, min_val=0, max_val=(B * T - PER_SLOT * P)), PER_SLOT * P)
                        pool.tensor_copy(state[:, at], xn_T[:, at]).then_inc(intake_state, 1)
                    if last and e >= 1:
                        pool.wait_ge(ema_step, EMA_STEPS * HALVES * (B - 1) + 1)
                        for f in range(0, B // 2) if e == 1 else range(B // 2, B - 1):
                            pool.wait_ge(added, E * k)
                            pool.tensor_tensor(state[:, tokens(f)], state[:, tokens(f)], attn_T[:, tokens(f)],
                                               ALU.add).then_inc(final_T, 1)
                    pool.wait_ge(combined, E * k + e + 1)
                    wait(pool, added, E * k + e)
                    at = tokens_after_wait(b)
                    pool.tensor_tensor(state[:, at], state[:, at], weighted[:, e, :],
                                       ALU.add).then_inc(added, 1)

            run_slots(pool, slot)
            pool.wait_ge(ema_step, EMA_STEPS * (SLOTS // 2) + 1)
            pool.wait_ge(added, E * SLOTS - 1)
            pool.tensor_tensor(state[:, tokens(B - 1)], state[:, tokens(B - 1)], attn_T[:, tokens(B - 1)],
                               ALU.add).then_inc(added, 1)

        @block.scalar
        def _(act):
            act.dma_start(w1_raw[:, 0], W1[0]).then_inc(w1_in[0], 16)
            act.dma_start(rows[0:E * FC, :], b1.rearrange("e (c p) -> (e c) p", p=P)).then_inc(rows_in, 16)
            act.dma_start(rows[E * FC:E * FC + E, :], b2).then_inc(rows_in, 16)
            act.dma_start(rows[E * FC + E:ROWS, :], omega.rearrange("(o p) -> o p", o=1)).then_inc(rows_in, 16)
            act.dma_start(wg_raw[:], Wg.rearrange("r h e -> h r e")).then_inc(gate_in, 16)
            act.dma_start(bg_bc[:].rearrange("p r e -> p (r e)"),
                          bg.rearrange("r e -> (r e)").partition_broadcast(P)).then_inc(gate_in, 16)
            for b, v in enumerate((delta, alpha, beta)):
                act.dma_start(ema_in[:, b, :], v.rearrange("d n o -> d (n o)")).then_inc(ema_coef_in, 16)
            act.dma_start(ema_in[:, 3, :], gamma).then_inc(ema_coef_in, 16)
            def split_weights_hi(e):
                act.wait_ge(w1_in[e], 16)
                nc.scalar.copy(w1_hi[:, e], w1_raw[:, e]).then_inc(w_hi, 1)
                act.wait_ge(w2_in[e], 16)
                nc.scalar.copy(w2_hi[:, e], w2_raw[:, e]).then_inc(w_hi, 1)

            def early_T(b):
                act.wait_ge(xnT_psum, b + 1)
                if b == 0:
                    act.wait_ge(cur_ready, 1)
                nc.scalar.copy(xn_T[:, tokens(b)], y[:, b, :]).then_inc(xnT_ready, 1)
                nc.scalar.copy(state[:, tokens(b)], y[:, b, :]).then_inc(state_ready, 1)

            split_weights_hi(0)
            act.wait_ge(cols_psum, 1)
            nc.scalar.copy(cols[:], misc[:, 0, 0:ROWS]).then_inc(cols_ready, 1)
            split_weights_hi(1)
            early_T(0)
            early_T(1)
            act.wait_ge(ema_coef_in, 16 * 4)
            nc.scalar.activation(ema_e[:], ema_in[:, 0:2, :], ACT.Exp, scale=-1.0).then_inc(ema_exp, 1)
            nc.scalar.activation(warm[:], ident[:, 0:1], ACT.Gelu_apprx_tanh)

            def gate_tanh_of(k):
                act.wait_ge(gate_step, GATE_STEPS * (k + 1))
                nc.scalar.activation(gate_tanh[:], gate_arg[:], ACT.Tanh).then_inc(tanh_done, 1)

            gate_tanh_of(0)

            def slot(k, parity, first=False, last=False, intake=False):
                for j in range(STEPS):
                    act.wait_ge(z_full, STEPS * k + j + 1)
                    nc.scalar.activation(z[:, j % ZR, :], z[:, j % ZR, :], ACT.Gelu_apprx_tanh,
                                         bias=b1_col[:, j:j + 1]).then_inc(gelu_done, 1)
                    if j == 11 and parity == 1:
                        c = (k - 1) // 2
                        act.wait_ge(ema_step, EMA_STEPS * (c + 1))
                        nc.scalar.activation(pre_tanh[:], pre[:], ACT.Tanh).then_inc(pre_tanh_done, 1)
                    if j == TANH_AT and not last:
                        gate_tanh_of(k + 1)
                    if j in HI_ON_ACT:
                        act.wait_ge(gelu_done, STEPS * k + j + 1)
                        nc.scalar.copy(h_hi[:, j % ZR, :], z[:, j % ZR, :]).then_inc(hi_act, 1)
                    if first and j in (1, 5):
                        split_weights_hi(2 + j // 4)

            act.wait_ge(cols_ready, 1)
            run_slots(act, slot)

        @block.vector
        def _(dve):
            def ln_stats(b):
                t0 = b * TILES

                def sums():
                    dve.wait_ge(x_in[min(b, EARLY)], 16)
                    for t in range(t0, t0 + TILES):
                        ins = dve.bn_stats(bn[:, t, :], x_tok[:, t, :])
                    ins.then_inc(stats, 1)

                def moments():
                    dve.wait_ge(stats, 3 * b + 1)
                    for t in range(t0, t0 + TILES):
                        ins = dve.bn_aggr(mv[:, t, :], bn[:, t, :])
                    ins.then_inc(stats, 1)
                    dve.wait_ge(stats, 3 * b + 2)
                    dve.tensor_scalar(var_eps[:, t0:t0 + TILES], mv[:, t0:t0 + TILES, 1], LN_EPS, None,
                                      ALU.add).then_inc(stats, 1)

                return [sums, moments]

            def ln_rsqrt(b0, b1, n0):
                at = slice(b0 * TILES, b1 * TILES)

                def guess():
                    dve.wait_ge(stats, 3 * b1)
                    dve.tensor_scalar(half_bits[:, at], var_eps[:, at].bitcast(I32), 1, None,
                                      ALU.logical_shift_right).then_inc(rstd_step, 1)
                    dve.wait_ge(rstd_step, n0 + 1)
                    dve.tensor_scalar(rstd[:, at].bitcast(I32), half_bits[:, at], -1.0, float(RSQRT_MAGIC),
                                      ALU.mult, ALU.add).then_inc(rstd_step, 1)

                def newton_step(i):
                    def op():
                        n = n0 + 2 + 3 * i
                        dve.wait_ge(rstd_step, n)
                        dve.scalar_tensor_tensor(out=newton[:, at], in0=rstd[:, at], scalar=-0.5, in1=rstd[:, at],
                                                 op0=ALU.mult, op1=ALU.mult).then_inc(rstd_step, 1)
                        dve.wait_ge(rstd_step, n + 1)
                        dve.tensor_tensor(newton[:, at], newton[:, at], var_eps[:, at],
                                          ALU.mult).then_inc(rstd_step, 1)
                        dve.wait_ge(rstd_step, n + 2)
                        dve.scalar_tensor_tensor(out=rstd[:, at], in0=newton[:, at], scalar=1.5, in1=rstd[:, at],
                                                 op0=ALU.add, op1=ALU.mult).then_inc(rstd_step, 1)
                    return op

                return [guess] + [newton_step(i) for i in range(NEWTON)]

            RSQRT_STEPS = 2 + 3 * NEWTON

            def ln_apply(b):
                dve.wait_ge(rstd_step, RSQRT_STEPS * (b + 1))
                for t in range(TILES):
                    n = b * TILES + t
                    ins = dve.tensor_scalar(xn_early[:, b, t, :], x_tok[:, n, :], mv[:, n, 0:1],
                                            rstd[:, n:n + 1], ALU.subtract, ALU.mult)
                ins.then_inc(xn_ready, 1)

            for b in range(EARLY):
                for op in ln_stats(b) + ln_rsqrt(b, b + 1, RSQRT_STEPS * b):
                    op()
                ln_apply(b)
                if b == 0:
                    dve.wait_ge(xnT_psum, 1)
                    dve.tensor_copy(cur_hi[:, 0, :], y[:, 0, :]).then_inc(cur_hi_ready, 1)
                    dve.wait_ge(cur_hi_ready, 1)
                    dve.tensor_tensor(cur_lo[:, 0, :], y[:, 0, :], cur_hi[:, 0, :].bitcast(F32),
                                      ALU.subtract).then_inc(cur_ready, 1)
            dve.wait_ge(gate_in, 32)
            dve.tensor_copy(wg_split[:, :, 0, :], wg_raw[:]).then_inc(wg_ready, 1)
            dve.wait_ge(wg_ready, 1)
            dve.tensor_tensor(wg_split[:, :, 1, :], wg_raw[:], wg_split[:, :, 0, :].bitcast(F32),
                              ALU.subtract).then_inc(wg_ready, 1)
            def ema_coefficients():
                dve.wait_ge(ema_exp, 1)
                dve.tensor_scalar(ema_s[:], ema_e[:], 1.0, None, ALU.add).then_inc(ema_chain, 1)
                dve.wait_ge(ema_chain, 1)
                dve.reciprocal(ema_e[:], ema_s[:]).then_inc(ema_chain, 1)
                dve.wait_ge(ema_chain, 2)
                dve.tensor_tensor(ema_pa[:], ema_e[:, 0, :], ema_e[:, 1, :], ALU.mult).then_inc(ema_chain, 1)
                dve.wait_ge(ema_chain, 3)
                dve.tensor_scalar(ema_q[:], ema_pa[:], -1.0, 1.0, ALU.mult, ALU.add).then_inc(q_ready, 1)
                dve.tensor_tensor(ema_c[:, 0, :], ema_e[:, 0, :], ema_in[:, 2, :], ALU.mult).then_inc(ema_chain, 1)
                dve.tensor_scalar(ema_c[:, 1, :], ema_in[:, 3, :], EMA_SCALE, 0.5, ALU.mult,
                                  ALU.mult).then_inc(ema_chain, 1)
                dve.wait_ge(ema_chain, 5)
                dve.tensor_tensor(ema_c[:, 2, :], ema_c[:, 0, :], ema_c[:, 1, :], ALU.mult).then_inc(ema_chain, 1)
                dve.wait_ge(cols_ready, 1)
                dve.tensor_scalar(omega_half[:], omega_col, 0.5, None, ALU.mult).then_inc(ema_chain, 1)

            def gate_ops(k, rnd):
                g0 = GATE_STEPS * k

                def logits_a():
                    dve.wait_ge(lg_psum, k + 1)
                    bias = bg_bc[:, bass.ds(rnd, 1), :].broadcast_to([P, TILES, E])
                    dve.tensor_tensor(lg[:], lg_ps[:, :, 0, :], bias, ALU.add).then_inc(gate_step, 1)

                def logits_b():
                    dve.wait_ge(gate_step, g0 + 1)
                    dve.tensor_tensor(lg[:], lg_ps[:, :, 1, :], lg[:], ALU.add).then_inc(gate_step, 1)

                def top():
                    dve.wait_ge(gate_step, g0 + 2)
                    dve.tensor_reduce(top1[:], lg[:], AX_X, ALU.max).then_inc(gate_step, 1)

                def rank_beats():
                    other = lg[:].unsqueeze(2).broadcast_to([P, TILES, E, E])
                    mine = lg[:].unsqueeze(3).broadcast_to([P, TILES, E, E])
                    dve.tensor_tensor(beats[:], other, mine, ALU.is_gt).then_inc(gate_step, 1)

                def rank_ties():
                    other = lg[:].unsqueeze(2).broadcast_to([P, TILES, E, E])
                    mine = lg[:].unsqueeze(3).broadcast_to([P, TILES, E, E])
                    dve.tensor_tensor(ties[:], other, mine, ALU.is_equal).then_inc(gate_step, 1)

                def rank_low_ties():
                    dve.wait_ge(gate_step, g0 + 5)
                    dve.tensor_tensor(ties[:], ties[:], lower[:].unsqueeze(1).broadcast_to([P, TILES, E, E]),
                                      ALU.mult).then_inc(gate_step, 1)

                def rank_all():
                    dve.wait_ge(gate_step, g0 + 6)
                    dve.tensor_tensor(beats[:], beats[:], ties[:], ALU.add).then_inc(gate_step, 1)

                def ranks():
                    dve.wait_ge(gate_step, g0 + 7)
                    dve.tensor_reduce(rank[:], beats[:], AX_X, ALU.add).then_inc(gate_step, 1)

                def distance():
                    dve.tensor_tensor(below[:], lg[:], top1[:].unsqueeze(2).broadcast_to([P, TILES, E]),
                                      ALU.subtract).then_inc(gate_step, 1)

                def selected():
                    dve.wait_ge(gate_step, g0 + 8)
                    dve.tensor_scalar(half_sel[:], rank[:], 2.0, 0.5, ALU.is_lt, ALU.mult).then_inc(gate_step, 1)

                def selected_distance():
                    dve.wait_ge(gate_step, g0 + 10)
                    dve.tensor_tensor(below_sel[:], below[:], half_sel[:], ALU.mult).then_inc(gate_step, 1)

                def distance_of_two():
                    dve.wait_ge(gate_step, g0 + 11)
                    dve.tensor_reduce(gap[:], below_sel[:], AX_X, ALU.add).then_inc(gap_done, 1)

                def softmax_arg():
                    dve.wait_ge(gap_done, k + 1)
                    dve.tensor_tensor(gate_arg[:], below[:], gap[:].unsqueeze(2).broadcast_to([P, TILES, E]),
                                      ALU.subtract).then_inc(gate_step, 1)

                return [[logits_a, logits_b], [top, rank_beats, rank_ties], [rank_low_ties, rank_all],
                        [ranks, distance, selected], [selected_distance, distance_of_two, softmax_arg]]

            def gate_weights(k):
                dve.wait_ge(tanh_done, k + 1)
                dve.scalar_tensor_tensor(out=gate_w[:].rearrange("p e t -> p t e"), in0=gate_tanh[:], scalar=1.0,
                                         in1=half_sel[:], op0=ALU.add, op1=ALU.mult).then_inc(gate_ready, 1)

            def gate_T_copy(k):
                dve.wait_ge(gateT_psum, k + 1)
                wait(dve, rows_out, 16 * k)
                dve.tensor_copy(gate_T[:], misc[0:E * TILES, 0, 0:P]).then_inc(gateT_ready, 1)

            lg_ps = misc[:, 1, 0:TILES * 2 * E].rearrange("p (t s e) -> p t s e", t=TILES, s=2)
            for ops in gate_ops(0, 0):
                for op in ops:
                    op()
            gate_weights(0)
            gate_T_copy(0)

            def split_state_hi(k, b, parity):
                dve.tensor_copy(cur_hi[:, parity, :], state[:, tokens(b)]).then_inc(cur_hi_ready, 1)

            def combine(k, e, parity):
                dve.wait_ge(y_full, E * k + e + 1)
                dve.wait_ge(bc_in[e], 16 * (k + 1))
                if e < E - 1 or isinstance(k, int):
                    wait(dve, added, E * k + e + 1 - TR)
                dve.scalar_tensor_tensor(out=weighted[:, e, :], in0=y[:, e % YR, :], scalar=b2_col[:, e:e + 1],
                                         in1=gate_bc[:, parity, e, :], op0=ALU.add,
                                         op1=ALU.mult).then_inc(combined, 1)

            dve.memset(ema[:, :, 0:1], 0.0).then_inc(ema_step, 1)

            def attention(c):
                s0 = EMA_STEPS * c + 1
                chunk = tokens(c, CH)
                half = tokens(c % HALVES, CH)

                def scan(n):
                    def op():
                        dve.wait_ge(q_ready, 2)
                        dve.wait_ge(ema_step, s0)
                        dve.tensor_tensor_scan(ema[:, n, 1:1 + CH], q_tab[:, n, half], xn_T[:, chunk],
                                               ema[:, n, 0:1], ALU.mult, ALU.add).then_inc(ema_step, 1)
                    return op

                def residual():
                    dve.tensor_scalar(pre[:], xn_T[:, chunk], omega_half[:], None, ALU.mult).then_inc(ema_step, 1)

                def carry():
                    dve.wait_ge(ema_step, s0 + 2)
                    dve.tensor_copy(ema[:, :, 0:1], ema[:, :, CH:CH + 1]).then_inc(ema_step, 1)

                def mix(n):
                    def op():
                        dve.wait_ge(ema_step, s0 + 4 + n)
                        dve.scalar_tensor_tensor(out=pre[:], in0=ema[:, n, 1:1 + CH], scalar=ema_c[:, 2, n:n + 1],
                                                 in1=pre[:], op0=ALU.mult, op1=ALU.add).then_inc(ema_step, 1)
                    return op

                def silu():
                    dve.wait_ge(pre_tanh_done, c + 1)
                    dve.scalar_tensor_tensor(out=attn_T[:, chunk], in0=pre_tanh[:], scalar=1.0, in1=pre[:],
                                             op0=ALU.add, op1=ALU.mult).then_inc(ema_step, 1)

                return [[scan(0)], [scan(1)], [residual, carry], [mix(0)], [mix(1)], [silu]]

            def slot(k, parity, first=False, last=False, intake=False):
                extra = {}
                if first:
                    for b in range(EARLY, B):
                        extra.setdefault(2 * b - 3, []).append(ln_stats(b)[0])
                        extra.setdefault(2 * b - 2, []).append(ln_stats(b)[1])
                    guess, *newton_steps = ln_rsqrt(EARLY, B, RSQRT_STEPS * EARLY)
                    extra.setdefault(13, []).append(guess)
                    extra[14] = newton_steps[:1]
                    extra[15] = newton_steps[1:]
                    extra[0] = [ema_coefficients]
                if last:
                    for b in range(B - 1):
                        extra.setdefault(min(10 + b, 15), []).append(lambda b=b: final_add(b))
                if not last:
                    nxt, rnd = block_of(k + 1, 1 - parity)

                    def next_state():
                        if first:
                            dve.wait_ge(state_ready, 2)
                        else:
                            dve.wait_ge(added, E * k)
                            dve.wait_ge(z_full, STEPS * k)
                        split_state_hi(k + 1, nxt, 1 - parity)

                    extra.setdefault(3, []).append(next_state)
                    for n, ops in enumerate(gate_ops(k + 1, rnd)):
                        extra.setdefault(6 + n, []).extend(ops)
                    extra.setdefault(13, []).append(lambda: gate_weights(k + 1))
                    extra.setdefault(15, []).append(lambda: gate_T_copy(k + 1))
                if intake:
                    tile = EARLY * TILES + PER_SLOT * (k - 1)

                    def intake_apply():
                        if parity == 1:
                            dve.wait_ge(rstd_step, RSQRT_STEPS * (EARLY + 1))
                        for t in range(PER_SLOT):
                            ins = dve.tensor_scalar(xn_pair[:, t, :], x_tok[:, bass.ds(tile + t, 1), :],
                                                    mv[:, bass.ds(tile + t, 1), 0], rstd[:, bass.ds(tile + t, 1)],
                                                    ALU.subtract, ALU.mult)
                        ins.then_inc(intake_xn, 1)

                    def intake_copy():
                        dve.wait_ge(intake_psum, k)
                        dve.tensor_scalar(xn_T[:, intake_tokens(k)], misc[:, 1, 0:PER_SLOT * P], 1.0, None,
                                          ALU.mult).then_inc(intake_T, 1)

                    extra.setdefault(4, []).append(intake_apply)
                    extra.setdefault(11, []).append(intake_copy)
                if parity == 1:
                    for j, ops in zip((0, 2, 3, 5, 8, 14), attention((k - 1) // 2)):
                        extra.setdefault(j, []).extend(ops)
                for j in range(STEPS):
                    if j in HI_ON_DVE:
                        dve.wait_ge(gelu_done, STEPS * k + j + 1)
                        dve.tensor_copy(h_hi[:, j % ZR, :], z[:, j % ZR, :]).then_inc(hi_dve, 1)
                        n = HI_ON_DVE.index(j)
                        dve.wait_ge(hi_dve, len(HI_ON_DVE) * k + n + 1)
                    else:
                        dve.wait_ge(hi_act, len(HI_ON_ACT) * k + HI_ON_ACT.index(j) + 1)
                    dve.tensor_tensor(h_lo[:, j % ZR, :], z[:, j % ZR, :], h_hi[:, j % ZR, :].bitcast(F32),
                                      ALU.subtract).then_inc(lo_done, 1)
                    if j == 1 and not first:
                        combine(k - 1, E - 1, 1 - parity)
                    if j % FC == 2 and j > FC:
                        combine(k, j // FC - 1, parity)
                    for op in extra.get(j, []):
                        op()

            def final_add(b):
                dve.wait_ge(final_psum, b + 1)
                xs = x_tok[:, b * TILES:(b + 1) * TILES, :].rearrange("p t h -> p (t h)")
                src = misc[:, b % 2, :] if b < B - 1 else z[:, 0, :]
                dve.tensor_tensor(xs, src, xs, ALU.add).then_inc(final_ready, 1)

            run_slots(dve, slot)
            combine(SLOTS - 1, E - 1, 1)
            dve.wait_ge(combined, E * SLOTS)
            dve.wait_ge(added, E * SLOTS)
            dve.tensor_tensor(state[:, tokens(B - 1)], state[:, tokens(B - 1)], weighted[:, E - 1, :],
                              ALU.add).then_inc(final_T, 1)
            final_add(B - 1)

        @block.tensor
        def _(pe):
            pe.wait_ge(consts, 2)
            pe.wait_ge(rows_in, 48)
            pe.transpose(misc[:, 0, 0:ROWS], rows[:], ident[0:ROWS, 0:ROWS]).then_inc(cols_psum, 1)

            def early_transpose(b):
                pe.wait_ge(xn_ready, b + 1)
                for t in range(TILES):
                    ins = pe.transpose(y[:, b, t * P:(t + 1) * P], xn_early[:, b, t, :], ident[:])
                ins.then_inc(xnT_psum, 1)

            def intake_transpose(k):
                pe.wait_ge(intake_xn, k)
                pe.wait_ge(gate_step, GATE_STEPS * (k + 1) + 2)
                for t in range(PER_SLOT):
                    ins = pe.transpose(misc[:, 1, t * P:(t + 1) * P], xn_pair[:, t, :], ident[:])
                ins.then_inc(intake_psum, 1)

            def final_transpose(b):
                pe.wait_ge(final_T, b + 1)
                if 2 <= b < B - 1:
                    pe.wait_ge(final_ready, b - 1)
                dst = misc[:, b % 2, :] if b < B - 1 else z[:, 0, :]
                for t in range(TILES):
                    ins = pe.transpose(dst[:, t * P:(t + 1) * P],
                                       state[:, b * T + t * P:b * T + (t + 1) * P], ident[:])
                ins.then_inc(final_psum, 1)

            def logits(k, rnd, parity):
                pe.wait_ge(cur_ready, k + 1)
                if isinstance(k, int) and k == 0:
                    pe.wait_ge(wg_ready, 2)
                for t in range(TILES):
                    w = wg_split[:, bass.ds(rnd, 1), :, :].rearrange("p r s e -> p (r s e)")
                    dst = misc[:, 1, t * 2 * E:(t + 1) * 2 * E]
                    pe.matmul(dst, cur_hi[:, parity, t * P:(t + 1) * P], w, start=True, stop=False)
                    ins = pe.matmul(dst, cur_lo[:, parity, t * P:(t + 1) * P], w, start=False, stop=True)
                ins.then_inc(lg_psum, 1)

            def gate_transpose(k):
                pe.wait_ge(gate_ready, k + 1)
                if isinstance(k, int) and k == 0:
                    pe.wait_ge(cols_ready, 1)
                else:
                    pe.wait_ge(gateT_ready, k)
                pe.transpose(misc[0:E * TILES, 0, 0:P], gate_w[:].rearrange("p e t -> p (e t)"),
                             ident[:]).then_inc(gateT_psum, 1)

            def up(j, parity):
                e, c = divmod(j, FC)
                hi, lo = (w[:, e, c * P:(c + 1) * P] for w in (w1_hi, w1_lo))
                dst = z[:, j % ZR, :]
                pe.matmul(dst, hi, cur_hi[:, parity, :], start=True, stop=False)
                pe.matmul(dst, hi, cur_lo[:, parity, :], start=False, stop=False)
                pe.matmul(dst, lo, cur_hi[:, parity, :], start=False, stop=True).then_inc(z_full, 1)

            def down(k, j):
                e, c = divmod(j, FC)
                pe.wait_ge(lo_done, STEPS * k + j + 1)
                if c == 0:
                    wait(pe, combined, E * k + e + 1 - YR)
                hi, lo = (w[:, e, c, :] for w in (w2_hi, w2_lo))
                dst = y[:, e % YR, :]
                pe.matmul(dst, hi, h_hi[:, j % ZR, :], start=(c == 0), stop=False)
                pe.matmul(dst, hi, h_lo[:, j % ZR, :], start=False, stop=False)
                ins = pe.matmul(dst, lo, h_hi[:, j % ZR, :], start=False, stop=(c == FC - 1))
                if c == FC - 1:
                    ins.then_inc(y_full, 1)

            early_transpose(0)
            pe.wait_ge(cur_ready, 1)
            pe.wait_ge(w_lo, 1)
            for j in range(LAG):
                up(j, 0)
            early_transpose(1)
            logits(0, 0, 0)
            gate_transpose(0)
            pe.wait_ge(state_ready, EARLY)

            def slot(k, parity, first=False, last=False, intake=False):
                for j in range(STEPS):
                    if first and (j + LAG) % FC == 0 and j + LAG < STEPS:
                        pe.wait_ge(w_lo, 2 * ((j + LAG) // FC) + 1)
                    if first and j % FC == 0:
                        pe.wait_ge(w_lo, 2 * (j // FC) + 2)
                    if j + LAG < STEPS:
                        up(j + LAG, parity)
                    elif not last:
                        up(j + LAG - STEPS, 1 - parity)
                    down(k, j)
                    if j == 5 and not last:
                        logits(k + 1, block_of(k + 1, 1 - parity)[1], 1 - parity)
                    if j == 7 and intake:
                        intake_transpose(k)
                    if j == GATE_T_AT and not last:
                        gate_transpose(k + 1)
                    if last and j >= 9:
                        final_transpose(j - 9)

            run_slots(pe, slot)
            final_transpose(B - 1)


_INS = ['L0_attn_x', 'L0_attn_delta', 'L0_attn_alpha', 'L0_attn_beta', 'L0_attn_gamma', 'L0_attn_omega',
        'L0_ffn_Wg', 'L0_ffn_bg', 'L0_ffn_W1', 'L0_ffn_b1', 'L0_ffn_W2', 'L0_ffn_b2']
_OUTS = [((8, 512, 128), 'float32')]


def kernel(**inputs):
    import numpy as _np
    import concourse.bacc as _bacc
    from concourse import mybir as _mybir
    from concourse.bass_utils import run_bass_kernel_spmd as _run

    nc = _bacc.Bacc("TRN2", target_bir_lowering=False, num_devices=1)
    arrays, args = {}, []
    for name in _INS:
        a = _np.ascontiguousarray(inputs[name])
        arrays[f"in_{name}_dram"] = a
        args.append(nc.dram_tensor(f"in_{name}_dram", a.shape, _mybir.dt.from_np(a.dtype), kind="ExternalInput").ap())
    for i, (shape, dtype) in enumerate(_OUTS):
        dt = _mybir.dt.from_np(_np.dtype(dtype))
        args.append(nc.dram_tensor(f"out_{i}_dram", shape, dt, kind="ExternalOutput").ap())
    ema_and_routed_ffn_kernel(nc, *args)
    r = _run(nc, [arrays], core_ids=[0])
    got = tuple(r.results[0][f"out_{i}_dram"] for i in range(len(_OUTS)))
    return got[0]
```

```python
from contextlib import ExitStack

import concourse.bass as bass
from concourse import mybir

F32 = mybir.dt.float32
F32R = mybir.dt.float32r
I32 = mybir.dt.int32
ALU = mybir.AluOpType
ACT = mybir.ActivationFunctionType
AX_X = mybir.AxisListType.X


def ema_and_routed_ffn_kernel(nc, x, delta, alpha, beta, gamma, omega, Wg, bg, W1, b1, W2, b2, out):
    B, T, H = x.shape
    R, _, E = Wg.shape
    F = W1.shape[2]
    N = delta.shape[1]
    P = 128
    FC = F // P
    STEPS = E * FC
    TILES = T // P
    NTILES = B * TILES
    PAIRS = B // 2
    SLOTS = B * R
    LAG = 3
    ZR = 4
    YR = 2
    TR = 4
    CH = B * T // (SLOTS // 2)
    HALVES = T // CH
    LN_EPS = 1e-05
    RSQRT_MAGIC = 0x5F3759DF
    NEWTON = 3
    EARLY = 2
    PER_SLOT = 2
    INTAKE_SLOTS = (B - EARLY) * TILES // PER_SLOT
    EMA_SCALE = (1.0 / N) ** 0.5
    ROWS = E * FC + E + 1
    assert INTAKE_SLOTS % 2 == 0 and EARLY == 2
    assert H == P and T == 512 and SLOTS % 2 == 0 and HALVES == 2 and STEPS == 16
    HI_ON_DVE = (3, 12)
    TANH_AT = 12
    GATE_T_AT = 13
    STATS_AT = (5, 6, 7)
    RSQRT_AT = (8, 9, 11, 12, 13, 15)
    EARLY_T_AT = 1
    HI_BY_ACT = 4
    FINAL_AT = 3
    HI_ON_ACT = [j for j in range(STEPS) if j not in HI_ON_DVE]

    x_v = x.rearrange("b (t p) h -> b p t h", p=P)
    out_v = out.rearrange("b (t p) h -> b p t h", p=P)

    with ExitStack() as ctx:
        def sb(name, shape, dt=F32):
            return ctx.enter_context(nc.sbuf_tensor(name, shape, dt))

        def sem(name):
            return ctx.enter_context(nc.semaphore(name))

        x_tok = sb("x_tok", [P, NTILES, H])
        xn_early = sb("xn_early", [P, EARLY, TILES, H])
        xn_pair = sb("xn_pair", [P, PER_SLOT, H])
        xn_T = sb("xn_T", [P, B * T])
        state = sb("state", [P, B * T])
        attn_T = sb("attn_T", [P, B * T])
        w1_raw = sb("w1_raw", [P, E, F])
        w2_raw = sb("w2_raw", [P, E, FC, H])
        w1_hi = sb("w1_hi", [P, E, F], F32R)
        w1_lo = sb("w1_lo", [P, E, F], F32R)
        w2_hi = sb("w2_hi", [P, E, FC, H], F32R)
        w2_lo = sb("w2_lo", [P, E, FC, H], F32R)
        wg_raw = sb("wg_raw", [P, R, E])
        wg_split = sb("wg_split", [P, R, 2, E], F32R)
        bg_bc = sb("bg_bc", [P, R, E])
        rows = sb("rows", [ROWS, P])
        cols = sb("cols", [P, ROWS])
        cur_hi = sb("cur_hi", [P, 2, T], F32R)
        cur_lo = sb("cur_lo", [P, 2, T], F32R)
        h_hi = sb("h_hi", [P, ZR, T], F32R)
        h_lo = sb("h_lo", [P, ZR, T], F32R)
        lg = sb("lg", [P, TILES, E])
        top1 = sb("top1", [P, TILES])
        beats = sb("beats", [P, TILES, E, E])
        ties = sb("ties", [P, TILES, E, E])
        rank = sb("rank", [P, TILES, E])
        half_sel = sb("half_sel", [P, TILES, E])
        below = sb("below", [P, TILES, E])
        below_sel = sb("below_sel", [P, TILES, E])
        gap = sb("gap", [P, TILES])
        gate_arg = sb("gate_arg", [P, TILES, E])
        gate_tanh = sb("gate_tanh", [P, TILES, E])
        gate_w = sb("gate_w", [P, E, TILES])
        gate_T = sb("gate_T", [E * TILES, P])
        gate_rows = nc.dram_tensor("gate_rows", [E, T], F32, kind="Internal").ap()
        gate_bc = sb("gate_bc", [P, 2, E, T])
        weighted = sb("weighted", [P, TR, T])
        ident = sb("ident", [P, P])
        lower = sb("lower", [P, E, E])
        STAT_TILES = (EARLY + 1) * TILES
        bn = sb("bn", [P, STAT_TILES, 6])
        mv = sb("mv", [P, STAT_TILES, 2])
        var_eps = sb("var_eps", [P, STAT_TILES])
        half_bits = sb("half_bits", [P, STAT_TILES], I32)
        newton = sb("newton", [P, STAT_TILES])
        rstd = sb("rstd", [P, STAT_TILES])
        ema_in = sb("ema_in", [P, 4, N])
        ema_e = sb("ema_e", [P, 2, N])
        ema_s = sb("ema_s", [P, 2, N])
        ema_pa = sb("ema_pa", [P, N])
        ema_q = sb("ema_q", [P, N])
        ema_c = sb("ema_c", [P, 3, N])
        omega_half = sb("omega_half", [P, 1])
        q_tab = sb("q_tab", [P, N, T])
        zeros = sb("zeros", [P, T])
        ema = sb("ema", [P, N, 1 + CH])
        pre = sb("pre", [P, CH])
        pre_tanh = sb("pre_tanh", [P, CH])
        warm = sb("warm", [P, 1])

        z = ctx.enter_context(nc.psum_tensor("z", [P, ZR, T], F32))
        y = ctx.enter_context(nc.psum_tensor("y", [P, YR, T], F32))
        misc = ctx.enter_context(nc.psum_tensor("misc", [P, 2, T], F32))
        b1_col = cols[:, 0:E * FC]
        b2_col = cols[:, E * FC:E * FC + E]
        omega_col = cols[:, E * FC + E:ROWS]

        x_in = [sem(f"x_in{b}") for b in range(EARLY + 1)]
        w1_in = [sem(f"w1_in{e}") for e in range(E)]
        w2_in = [sem(f"w2_in{e}") for e in range(E)]
        rows_in = sem("rows_in")
        gate_in = sem("gate_in")
        ema_coef_in = sem("ema_coef_in")
        ema_out_in = sem("ema_out_in")
        out_done = sem("out_done")
        consts = sem("consts")
        stats = sem("stats")
        rstd_step = sem("rstd_step")
        xn_ready = sem("xn_ready")
        intake_xn = sem("intake_xn")
        intake_psum = sem("intake_psum")
        intake_T = sem("intake_T")
        intake_state = sem("intake_state")
        xnT_psum = sem("xnT_psum")
        xnT_ready = sem("xnT_ready")
        state_ready = sem("state_ready")
        cols_psum = sem("cols_psum")
        cols_ready = sem("cols_ready")
        w_hi = sem("w_hi")
        w_lo = sem("w_lo")
        wg_ready = sem("wg_ready")
        ema_exp = sem("ema_exp")
        ema_chain = sem("ema_chain")
        q_ready = sem("q_ready")
        z_full = sem("z_full")
        gelu_done = sem("gelu_done")
        hi_act = sem("hi_act")
        hi_dve = sem("hi_dve")
        lo_done = sem("lo_done")
        y_full = sem("y_full")
        combined = sem("combined")
        added = sem("added")
        cur_hi_ready = sem("cur_hi_ready")
        cur_ready = sem("cur_ready")
        lg_psum = sem("lg_psum")
        gate_step = sem("gate_step")
        gap_done = sem("gap_done")
        tanh_done = sem("tanh_done")
        gate_ready = sem("gate_ready")
        gateT_psum = sem("gateT_psum")
        gateT_ready = sem("gateT_ready")
        rows_out = sem("rows_out")
        bc_in = [sem(f"bc_in{e}") for e in range(E)]
        ema_step = sem("ema_step")
        pre_tanh_done = sem("pre_tanh_done")
        final_T = sem("final_T")
        final_psum = sem("final_psum")
        final_ready = sem("final_ready")

        GATE_STEPS = 12
        EMA_STEPS = 7

        def wait(eng, s, value):
            if not isinstance(value, int) or value > 0:
                eng.wait_ge(s, value)

        def block_of(k, parity):
            turn = (k - parity) // 2
            return 2 * (turn // R) + parity, turn % R

        def tokens(b, size=T):
            return bass.ds(b * size, size)

        def intake_tokens(k):
            return bass.ds((EARLY * TILES + PER_SLOT * (k - 1)) * P, PER_SLOT * P)

        def run_slots(eng, slot):
            slot(0, 0, first=True)
            with eng.Fori(0, INTAKE_SLOTS // 2 - 1) as i:
                slot(2 * i + 1, 1, intake=True)
                slot(2 * i + 2, 0, intake=True, ahead=True)
            with eng.Fori(INTAKE_SLOTS // 2 - 1, INTAKE_SLOTS // 2) as i:
                slot(2 * i + 1, 1, intake=True)
                slot(2 * i + 2, 0, intake=True)
            with eng.Fori(INTAKE_SLOTS // 2, SLOTS // 2 - 1) as i:
                slot(2 * i + 1, 1)
                slot(2 * i + 2, 0)
            slot(SLOTS - 1, 1, last=True)

        block = ctx.enter_context(nc.Block())

        @block.sync
        def _(sp):
            def load_x(b):
                sp.dma_start(x_tok[:, b * TILES:(b + 1) * TILES, :], x_v[b]).then_inc(x_in[b], 16)

            def load_w2(e):
                sp.dma_start(w2_raw[:, e], W2[e].rearrange("(c p) h -> p c h", p=P)).then_inc(w2_in[e], 16)

            load_x(0)
            load_w2(0)
            load_x(1)
            for e in range(1, E):
                sp.dma_start(w1_raw[:, e], W1[e]).then_inc(w1_in[e], 16)
                load_w2(e)
            sp.wait_ge(rows_in, 48)
            sp.dma_start(x_tok[:, EARLY * TILES:NTILES, :].rearrange("p (b t) h -> p b t h", t=TILES),
                         x[EARLY:B].rearrange("b (t p) h -> p b t h", p=P)).then_inc(x_in[EARLY], 16)

            count_regs = [sp.alloc_register(f"count{n}") for n in range(4)]

            def broadcast_gate(k, parity):
                counts = (k + 1, 16 * k, E * (k - 1), 16 * (k + 1))
                if not isinstance(k, int):
                    for register, count in zip(count_regs, counts):
                        sp.reg_mov(register, count)
                    counts = [sp.snap(register) for register in count_regs]
                transposed, last_in, used, in_dram = counts
                sp.wait_ge(gateT_ready, transposed)
                if not isinstance(k, int) or k > 0:
                    for e in range(E):
                        sp.wait_ge(bc_in[e], last_in)
                sp.dma_start(gate_rows.rearrange("e (t p) -> (e t) p", p=P), gate_T[:]).then_inc(rows_out, 16)
                if not isinstance(k, int) or k > 1:
                    sp.wait_ge(combined, used)
                sp.wait_ge(rows_out, in_dram)
                for e in range(E):
                    sp.dma_start(gate_bc[:, parity, e, :],
                                 gate_rows[e].partition_broadcast(P)).then_inc(bc_in[e], 16)

            broadcast_gate(0, 0)
            broadcast_gate(1, 1)
            with sp.Fori(1, SLOTS // 2) as i:
                broadcast_gate(2 * i, 0)
                broadcast_gate(2 * i + 1, 1)
            for b in range(B - 1):
                sp.wait_ge(final_ready, b + 1)
                sp.dma_start(out_v[b], x_tok[:, b * TILES:(b + 1) * TILES, :]).then_inc(out_done, 16)
            for half in range(HALVES):
                sp.wait_ge(final_ready, B + half)
                t0 = half * TILES // HALVES
                t1 = t0 + TILES // HALVES
                sp.dma_start(out_v[B - 1, :, t0:t1, :],
                             x_tok[:, (B - 1) * TILES + t0:(B - 1) * TILES + t1, :]).then_inc(out_done, 16)
            sp.wait_ge(out_done, 16 * (B - 1 + HALVES))

        @block.gpsimd
        def _(pool):
            start_reg = pool.alloc_register("start_reg")
            pool.memset(ident[:], 0.0).then_inc(consts, 1)
            pool.wait_ge(consts, 1)
            pool.affine_select(out=ident[:], in_=ident[:], compare_op=ALU.not_equal, fill=1.0, base=0,
                               pattern=[[-1, P]], channel_multiplier=1).then_inc(consts, 1)
            pool.dma_start(wg_raw[:], Wg.rearrange("r h e -> h r e")).then_inc(gate_in, 16)
            pool.dma_start(bg_bc[:].rearrange("p r e -> p (r e)"),
                           bg.rearrange("r e -> (r e)").partition_broadcast(P)).then_inc(gate_in, 16)
            pool.dma_start(ema_in[:, 2, :], beta.rearrange("d n o -> d (n o)")).then_inc(ema_out_in, 16)
            pool.dma_start(ema_in[:, 3, :], gamma).then_inc(ema_out_in, 16)
            pool.memset(lower[:], 0.0).then_inc(consts, 1)
            pool.wait_ge(consts, 3)
            pool.affine_select(out=lower[:], in_=lower[:], compare_op=ALU.is_ge, fill=1.0, base=0,
                               pattern=[[-1, E], [1, E]], channel_multiplier=0).then_inc(consts, 1)
            pool.memset(zeros[:], 0.0).then_inc(consts, 1)

            def tokens_after_wait(b):
                if isinstance(b, int):
                    return tokens(b)
                pool.reg_mov(start_reg, b * T)
                return bass.ds(pool.snap(start_reg, min_val=0, max_val=(B - 1) * T), T)

            def split_state(k, b, parity):
                pool.wait_ge(cur_hi_ready, k + 1)
                at = tokens_after_wait(b)
                pool.tensor_tensor(cur_lo[:, parity, :], state[:, at],
                                   cur_hi[:, parity, :].bitcast(F32), ALU.subtract).then_inc(cur_ready, 1)

            def split_weights(raw, hi, lo, e, n, raw_in):
                if n > HI_BY_ACT:
                    pool.wait_ge(raw_in[e], 16)
                    pool.tensor_copy(hi[:, e], raw[:, e]).then_inc(w_hi, 1)
                pool.wait_ge(w_hi, n)
                pool.tensor_tensor(lo[:, e], raw[:, e], hi[:, e].bitcast(F32), ALU.subtract).then_inc(w_lo, 1)

            for e in range(E):
                split_weights(w1_raw, w1_hi, w1_lo, e, 2 * e + 1, w1_in)
                if e < E - 1:
                    split_weights(w2_raw, w2_hi, w2_lo, e, 2 * e + 2, w2_in)

            def scan_multiplier():
                pool.wait_ge(consts, 5)
                pool.wait_ge(q_ready, 1)
                for n in range(N):
                    pool.tensor_scalar(q_tab[:, n, :], zeros[:], ema_q[:, n:n + 1], None, ALU.add).then_inc(consts, 1)
                pool.wait_ge(consts, 5 + N)
                pool.memset(q_tab[:, :, 0:1], 0.0).then_inc(q_ready, 1)

            def slot(k, parity, first=False, last=False, intake=False, ahead=False):
                b, _ = block_of(k, parity)
                def add_attention(f):
                    pool.tensor_tensor(state[:, tokens(f)], state[:, tokens(f)], attn_T[:, tokens(f)],
                                       ALU.add).then_inc(final_T, 1)

                if last:
                    pool.wait_ge(ema_step, EMA_STEPS * HALVES * (B - 1) + 1)
                    pool.wait_ge(added, E * R * (B - 2))
                    for f in range(B - 2):
                        add_attention(f)
                if not first:
                    prev, _ = block_of(k - 1, 1 - parity)
                    pool.wait_ge(combined, E * k)
                    pool.wait_ge(added, E * k - 1)
                    at = tokens_after_wait(prev)
                    pool.tensor_tensor(state[:, at], state[:, at], weighted[:, E - 1, :],
                                       ALU.add).then_inc(added, 1)
                if last:
                    pool.wait_ge(added, E * k)
                    add_attention(B - 2)
                if not last:
                    nxt, _ = block_of(k + 1, 1 - parity)
                    split_state(k + 1, nxt, 1 - parity)
                if first:
                    split_weights(w2_raw, w2_hi, w2_lo, E - 1, 2 * E, w2_in)
                    scan_multiplier()
                for e in range(E - 1):
                    if e == 2 and intake:
                        pool.wait_ge(intake_T, k)
                        pool.reg_mov(start_reg, (EARLY * TILES + PER_SLOT * (k - 1)) * P)
                        at = bass.ds(pool.snap(start_reg, min_val=0, max_val=(B * T - PER_SLOT * P)), PER_SLOT * P)
                        pool.tensor_copy(state[:, at], xn_T[:, at]).then_inc(intake_state, 1)
                    pool.wait_ge(combined, E * k + e + 1)
                    wait(pool, added, E * k + e)
                    at = tokens_after_wait(b)
                    pool.tensor_tensor(state[:, at], state[:, at], weighted[:, e, :],
                                       ALU.add).then_inc(added, 1)

            run_slots(pool, slot)
            pool.wait_ge(ema_step, EMA_STEPS * (SLOTS // 2) + 1)
            pool.wait_ge(added, E * SLOTS - 1)
            pool.tensor_tensor(state[:, tokens(B - 1)], state[:, tokens(B - 1)], attn_T[:, tokens(B - 1)],
                               ALU.add).then_inc(added, 1)

        @block.scalar
        def _(act):
            act.dma_start(w1_raw[:, 0], W1[0]).then_inc(w1_in[0], 16)
            for n, v in enumerate((delta, alpha)):
                act.dma_start(ema_in[:, n, :], v.rearrange("d n o -> d (n o)")).then_inc(ema_coef_in, 16)
            act.dma_start(rows[0:E * FC, :], b1.rearrange("e (c p) -> (e c) p", p=P)).then_inc(rows_in, 16)
            act.dma_start(rows[E * FC:E * FC + E, :], b2).then_inc(rows_in, 16)
            act.dma_start(rows[E * FC + E:ROWS, :], omega.rearrange("(o p) -> o p", o=1)).then_inc(rows_in, 16)

            def split_weights_hi(e):
                act.wait_ge(w1_in[e], 16)
                nc.scalar.copy(w1_hi[:, e], w1_raw[:, e]).then_inc(w_hi, 1)
                act.wait_ge(w2_in[e], 16)
                nc.scalar.copy(w2_hi[:, e], w2_raw[:, e]).then_inc(w_hi, 1)

            def early_T(b):
                act.wait_ge(xnT_psum, b + 1)
                if b == 0:
                    act.wait_ge(cur_ready, 1)
                nc.scalar.copy(xn_T[:, tokens(b)], y[:, b, :]).then_inc(xnT_ready, 1)
                nc.scalar.copy(state[:, tokens(b)], y[:, b, :]).then_inc(state_ready, 1)

            split_weights_hi(0)
            act.wait_ge(ema_coef_in, 16 * 2)
            nc.scalar.activation(ema_e[:], ema_in[:, 0:2, :], ACT.Exp, scale=-1.0).then_inc(ema_exp, 1)
            act.wait_ge(consts, 2)
            nc.scalar.activation(warm[:], ident[:, 0:1], ACT.Gelu_apprx_tanh)
            act.wait_ge(cols_psum, 1)
            nc.scalar.copy(cols[:], misc[:, 0, 0:ROWS]).then_inc(cols_ready, 1)
            split_weights_hi(1)
            early_T(0)

            def gate_tanh_of(k):
                act.wait_ge(gate_step, GATE_STEPS * (k + 1))
                nc.scalar.activation(gate_tanh[:], gate_arg[:], ACT.Tanh).then_inc(tanh_done, 1)

            def slot(k, parity, first=False, last=False, intake=False, ahead=False):
                for j in range(STEPS):
                    act.wait_ge(z_full, STEPS * k + j + 1)
                    nc.scalar.activation(z[:, j % ZR, :], z[:, j % ZR, :], ACT.Gelu_apprx_tanh,
                                         bias=b1_col[:, j:j + 1]).then_inc(gelu_done, 1)
                    if j == 11 and parity == 1:
                        c = (k - 1) // 2
                        act.wait_ge(ema_step, EMA_STEPS * (c + 1))
                        nc.scalar.activation(pre_tanh[:], pre[:], ACT.Tanh).then_inc(pre_tanh_done, 1)
                    if j == TANH_AT and not last:
                        gate_tanh_of(k + 1)
                    if j in HI_ON_ACT:
                        act.wait_ge(gelu_done, STEPS * k + j + 1)
                        nc.scalar.copy(h_hi[:, j % ZR, :], z[:, j % ZR, :]).then_inc(hi_act, 1)
                    if first and j == 0:
                        gate_tanh_of(0)
                    if first and j == EARLY_T_AT + 1:
                        early_T(1)

            act.wait_ge(cols_ready, 1)
            run_slots(act, slot)

        @block.vector
        def _(dve):
            def stat_columns(b):
                first_column = min(b, EARLY) * TILES if isinstance(b, int) else EARLY * TILES
                return range(first_column, first_column + TILES)

            def ln_stats(b):
                columns = stat_columns(b)

                def sums():
                    if isinstance(b, int):
                        dve.wait_ge(x_in[b], 16)
                    for t, column in enumerate(columns):
                        ins = dve.bn_stats(bn[:, column, :],
                                           x_tok[:, bass.ds(b * TILES + t, 1), :].rearrange("p o h -> p (o h)"))
                    ins.then_inc(stats, 1)

                def wait_for_sums():
                    dve.wait_ge(stats, 2 * b + 1)

                def moments():
                    for column in columns:
                        ins = dve.bn_aggr(mv[:, column, :], bn[:, column, :])
                    ins.then_inc(stats, 1)

                return [sums, wait_for_sums, moments]

            def ln_rsqrt(b):
                at = slice(stat_columns(b)[0], stat_columns(b)[0] + TILES)
                n0 = RSQRT_STEPS * b

                def add_eps():
                    dve.wait_ge(stats, 2 * b + 2)
                    dve.tensor_scalar(var_eps[:, at], mv[:, at, 1], LN_EPS, None, ALU.add).then_inc(rstd_step, 1)

                def half():
                    dve.wait_ge(rstd_step, n0 + 1)
                    dve.tensor_scalar(half_bits[:, at], var_eps[:, at].bitcast(I32), 1, None,
                                      ALU.logical_shift_right).then_inc(rstd_step, 1)

                def guess():
                    dve.wait_ge(rstd_step, n0 + 2)
                    dve.tensor_scalar(rstd[:, at].bitcast(I32), half_bits[:, at], -1.0, float(RSQRT_MAGIC),
                                      ALU.mult, ALU.add).then_inc(rstd_step, 1)

                def newton_step(i):
                    n = n0 + 3 + 3 * i

                    def square():
                        dve.wait_ge(rstd_step, n)
                        dve.scalar_tensor_tensor(out=newton[:, at], in0=rstd[:, at], scalar=-0.5, in1=rstd[:, at],
                                                 op0=ALU.mult, op1=ALU.mult).then_inc(rstd_step, 1)

                    def times_var():
                        dve.wait_ge(rstd_step, n + 1)
                        dve.tensor_tensor(newton[:, at], newton[:, at], var_eps[:, at],
                                          ALU.mult).then_inc(rstd_step, 1)

                    def update():
                        dve.wait_ge(rstd_step, n + 2)
                        dve.scalar_tensor_tensor(out=rstd[:, at], in0=newton[:, at], scalar=1.5, in1=rstd[:, at],
                                                 op0=ALU.add, op1=ALU.mult).then_inc(rstd_step, 1)

                    return [square, times_var, update]

                return [add_eps, half, guess] + [op for i in range(NEWTON) for op in newton_step(i)]

            RSQRT_STEPS = 3 + 3 * NEWTON

            def ln_apply(b):
                dve.wait_ge(rstd_step, RSQRT_STEPS * (b + 1))
                for t in range(TILES):
                    n = b * TILES + t
                    ins = dve.tensor_scalar(xn_early[:, b, t, :], x_tok[:, n, :], mv[:, n, 0:1],
                                            rstd[:, n:n + 1], ALU.subtract, ALU.mult)
                ins.then_inc(xn_ready, 1)

            for op in ln_stats(0) + ln_rsqrt(0):
                op()
            ln_apply(0)
            dve.wait_ge(gate_in, 32)
            dve.tensor_copy(wg_split[:, :, 0, :], wg_raw[:]).then_inc(wg_ready, 1)
            dve.wait_ge(wg_ready, 1)
            dve.tensor_tensor(wg_split[:, :, 1, :], wg_raw[:], wg_split[:, :, 0, :].bitcast(F32),
                              ALU.subtract).then_inc(wg_ready, 1)
            dve.wait_ge(xnT_psum, 1)
            dve.tensor_copy(cur_hi[:, 0, :], y[:, 0, :]).then_inc(cur_hi_ready, 1)
            dve.wait_ge(cur_hi_ready, 1)
            dve.tensor_tensor(cur_lo[:, 0, :], y[:, 0, :], cur_hi[:, 0, :].bitcast(F32),
                              ALU.subtract).then_inc(cur_ready, 1)

            def ema_coefficients():
                dve.wait_ge(ema_exp, 1)
                dve.wait_ge(ema_out_in, 32)
                dve.tensor_scalar(ema_s[:], ema_e[:], 1.0, None, ALU.add).then_inc(ema_chain, 1)
                dve.wait_ge(ema_chain, 1)
                dve.reciprocal(ema_e[:], ema_s[:]).then_inc(ema_chain, 1)
                dve.wait_ge(ema_chain, 2)
                dve.tensor_tensor(ema_pa[:], ema_e[:, 0, :], ema_e[:, 1, :], ALU.mult).then_inc(ema_chain, 1)
                dve.wait_ge(ema_chain, 3)
                dve.tensor_scalar(ema_q[:], ema_pa[:], -1.0, 1.0, ALU.mult, ALU.add).then_inc(q_ready, 1)
                dve.tensor_tensor(ema_c[:, 0, :], ema_e[:, 0, :], ema_in[:, 2, :], ALU.mult).then_inc(ema_chain, 1)
                dve.tensor_scalar(ema_c[:, 1, :], ema_in[:, 3, :], EMA_SCALE, 0.5, ALU.mult,
                                  ALU.mult).then_inc(ema_chain, 1)
                dve.wait_ge(ema_chain, 5)
                dve.tensor_tensor(ema_c[:, 2, :], ema_c[:, 0, :], ema_c[:, 1, :], ALU.mult).then_inc(ema_chain, 1)
                dve.wait_ge(cols_ready, 1)
                dve.tensor_scalar(omega_half[:], omega_col, 0.5, None, ALU.mult).then_inc(ema_chain, 1)

            def gate_ops(k, rnd):
                g0 = GATE_STEPS * k

                def logits_a():
                    dve.wait_ge(lg_psum, k + 1)
                    bias = bg_bc[:, bass.ds(rnd, 1), :].broadcast_to([P, TILES, E])
                    dve.tensor_tensor(lg[:], lg_ps[:, :, 0, :], bias, ALU.add).then_inc(gate_step, 1)

                def logits_b():
                    dve.wait_ge(gate_step, g0 + 1)
                    dve.tensor_tensor(lg[:], lg_ps[:, :, 1, :], lg[:], ALU.add).then_inc(gate_step, 1)

                def top():
                    dve.wait_ge(gate_step, g0 + 2)
                    dve.tensor_reduce(top1[:], lg[:], AX_X, ALU.max).then_inc(gate_step, 1)

                def rank_beats():
                    other = lg[:].unsqueeze(2).broadcast_to([P, TILES, E, E])
                    mine = lg[:].unsqueeze(3).broadcast_to([P, TILES, E, E])
                    dve.tensor_tensor(beats[:], other, mine, ALU.is_gt).then_inc(gate_step, 1)

                def rank_ties():
                    other = lg[:].unsqueeze(2).broadcast_to([P, TILES, E, E])
                    mine = lg[:].unsqueeze(3).broadcast_to([P, TILES, E, E])
                    dve.tensor_tensor(ties[:], other, mine, ALU.is_equal).then_inc(gate_step, 1)

                def rank_low_ties():
                    dve.wait_ge(gate_step, g0 + 5)
                    dve.tensor_tensor(ties[:], ties[:], lower[:].unsqueeze(1).broadcast_to([P, TILES, E, E]),
                                      ALU.mult).then_inc(gate_step, 1)

                def rank_all():
                    dve.wait_ge(gate_step, g0 + 6)
                    dve.tensor_tensor(beats[:], beats[:], ties[:], ALU.add).then_inc(gate_step, 1)

                def ranks():
                    dve.wait_ge(gate_step, g0 + 7)
                    dve.tensor_reduce(rank[:], beats[:], AX_X, ALU.add).then_inc(gate_step, 1)

                def distance():
                    dve.tensor_tensor(below[:], lg[:], top1[:].unsqueeze(2).broadcast_to([P, TILES, E]),
                                      ALU.subtract).then_inc(gate_step, 1)

                def selected():
                    dve.wait_ge(gate_step, g0 + 8)
                    dve.tensor_scalar(half_sel[:], rank[:], 2.0, 0.5, ALU.is_lt, ALU.mult).then_inc(gate_step, 1)

                def selected_distance():
                    dve.wait_ge(gate_step, g0 + 10)
                    dve.tensor_tensor(below_sel[:], below[:], half_sel[:], ALU.mult).then_inc(gate_step, 1)

                def distance_of_two():
                    dve.wait_ge(gate_step, g0 + 11)
                    dve.tensor_reduce(gap[:], below_sel[:], AX_X, ALU.add).then_inc(gap_done, 1)

                def softmax_arg():
                    dve.wait_ge(gap_done, k + 1)
                    dve.tensor_tensor(gate_arg[:], below[:], gap[:].unsqueeze(2).broadcast_to([P, TILES, E]),
                                      ALU.subtract).then_inc(gate_step, 1)

                return [[logits_a, logits_b], [top, rank_beats, rank_ties, rank_low_ties],
                        [rank_all, ranks, distance, selected],
                        [selected_distance, distance_of_two, softmax_arg]]

            def gate_weights(k):
                dve.wait_ge(tanh_done, k + 1)
                dve.scalar_tensor_tensor(out=gate_w[:].rearrange("p e t -> p t e"), in0=gate_tanh[:], scalar=1.0,
                                         in1=half_sel[:], op0=ALU.add, op1=ALU.mult).then_inc(gate_ready, 1)

            def gate_T_copy(k):
                dve.wait_ge(gateT_psum, k + 1)
                wait(dve, rows_out, 16 * k)
                dve.tensor_copy(gate_T[:], misc[0:E * TILES, 0, 0:P]).then_inc(gateT_ready, 1)

            lg_ps = misc[:, 1, 0:TILES * 2 * E].rearrange("p (t s e) -> p t s e", t=TILES, s=2)
            for op in ln_stats(1):
                op()
            dve.wait_ge(consts, 4)
            first_gate = [op for ops in gate_ops(0, 0) for op in ops]
            second_rsqrt = ln_rsqrt(1)
            by_turns = [op for pair in zip(first_gate, second_rsqrt) for op in pair]
            by_turns += first_gate[len(second_rsqrt):] + second_rsqrt[len(first_gate):]
            for op in by_turns:
                op()

            def split_state_hi(k, b, parity):
                dve.tensor_copy(cur_hi[:, parity, :], state[:, tokens(b)]).then_inc(cur_hi_ready, 1)

            def combine(k, e, parity):
                dve.wait_ge(y_full, E * k + e + 1)
                dve.wait_ge(bc_in[e], 16 * (k + 1))
                if e < E - 1 or isinstance(k, int):
                    wait(dve, added, E * k + e + 1 - TR)
                dve.scalar_tensor_tensor(out=weighted[:, e, :], in0=y[:, e % YR, :], scalar=b2_col[:, e:e + 1],
                                         in1=gate_bc[:, parity, e, :], op0=ALU.add,
                                         op1=ALU.mult).then_inc(combined, 1)

            dve.memset(ema[:, :, 0:1], 0.0).then_inc(ema_step, 1)

            def attention(c):
                s0 = EMA_STEPS * c + 1
                chunk = tokens(c, CH)
                half = tokens(c % HALVES, CH)

                def scan(n):
                    def op():
                        dve.wait_ge(q_ready, 2)
                        dve.wait_ge(ema_step, s0)
                        dve.tensor_tensor_scan(ema[:, n, 1:1 + CH], q_tab[:, n, half], xn_T[:, chunk],
                                               ema[:, n, 0:1], ALU.mult, ALU.add).then_inc(ema_step, 1)
                    return op

                def residual():
                    dve.tensor_scalar(pre[:], xn_T[:, chunk], omega_half[:], None, ALU.mult).then_inc(ema_step, 1)

                def carry():
                    dve.wait_ge(ema_step, s0 + 2)
                    dve.tensor_copy(ema[:, :, 0:1], ema[:, :, CH:CH + 1]).then_inc(ema_step, 1)

                def mix(n):
                    def op():
                        dve.wait_ge(ema_step, s0 + 4 + n)
                        dve.scalar_tensor_tensor(out=pre[:], in0=ema[:, n, 1:1 + CH], scalar=ema_c[:, 2, n:n + 1],
                                                 in1=pre[:], op0=ALU.mult, op1=ALU.add).then_inc(ema_step, 1)
                    return op

                def silu():
                    dve.wait_ge(pre_tanh_done, c + 1)
                    dve.scalar_tensor_tensor(out=attn_T[:, chunk], in0=pre_tanh[:], scalar=1.0, in1=pre[:],
                                             op0=ALU.add, op1=ALU.mult).then_inc(ema_step, 1)

                return [[scan(0)], [scan(1)], [residual, carry], [mix(0)], [mix(1)], [silu]]

            def slot(k, parity, first=False, last=False, intake=False, ahead=False):
                extra = {}
                if first:
                    extra[0] = [lambda: ln_apply(1)]
                    extra.setdefault(1, []).append(lambda: gate_weights(0))
                    extra.setdefault(2, []).insert(0, lambda: gate_T_copy(0))
                    extra.setdefault(2, []).append(ema_coefficients)
                if first or ahead:
                    coming = k // 2 + EARLY
                    for j, ops in zip(STATS_AT, ln_stats(coming)):
                        extra.setdefault(j, []).append(ops)
                    for n, op in enumerate(ln_rsqrt(coming)):
                        extra.setdefault(RSQRT_AT[n // 2], []).append(op)
                if last:
                    for b in range(B - 1):
                        extra.setdefault(FINAL_AT + 1 + b, []).append(lambda b=b: final_add(b))
                if not last:
                    nxt, rnd = block_of(k + 1, 1 - parity)

                    def next_state():
                        if first:
                            dve.wait_ge(state_ready, 2)
                        else:
                            dve.wait_ge(added, E * k)
                            dve.wait_ge(z_full, STEPS * k)
                        split_state_hi(k + 1, nxt, 1 - parity)

                    extra.setdefault(3, []).append(next_state)
                    for n, ops in enumerate(gate_ops(k + 1, rnd)):
                        extra.setdefault(7 + n, []).extend(ops)
                    extra.setdefault(13, []).append(lambda: gate_weights(k + 1))
                    extra.setdefault(15, []).append(lambda: gate_T_copy(k + 1))
                if intake:
                    tile = EARLY * TILES + PER_SLOT * (k - 1)
                    column = EARLY * TILES + PER_SLOT * (1 - parity)

                    def intake_apply():
                        if parity == 1:
                            dve.wait_ge(rstd_step, RSQRT_STEPS * ((k - 1) // 2 + EARLY + 1))
                        for t in range(PER_SLOT):
                            ins = dve.tensor_scalar(xn_pair[:, t, :], x_tok[:, bass.ds(tile + t, 1), :],
                                                    mv[:, column + t:column + t + 1, 0],
                                                    rstd[:, column + t:column + t + 1], ALU.subtract, ALU.mult)
                        ins.then_inc(intake_xn, 1)

                    def intake_copy():
                        dve.wait_ge(intake_psum, k)
                        dve.tensor_scalar(xn_T[:, intake_tokens(k)], misc[:, 1, 0:PER_SLOT * P], 1.0, None,
                                          ALU.mult).then_inc(intake_T, 1)

                    extra.setdefault(4, []).append(intake_apply)
                    extra.setdefault(11, []).append(intake_copy)
                if parity == 1:
                    for j, ops in zip((0, 2, 3, 5, 8, 14), attention((k - 1) // 2)):
                        extra.setdefault(j, []).extend(ops)
                for j in range(STEPS):
                    if j in HI_ON_DVE:
                        dve.wait_ge(gelu_done, STEPS * k + j + 1)
                        dve.tensor_copy(h_hi[:, j % ZR, :], z[:, j % ZR, :]).then_inc(hi_dve, 1)
                        n = HI_ON_DVE.index(j)
                        dve.wait_ge(hi_dve, len(HI_ON_DVE) * k + n + 1)
                    else:
                        dve.wait_ge(hi_act, len(HI_ON_ACT) * k + HI_ON_ACT.index(j) + 1)
                    dve.tensor_tensor(h_lo[:, j % ZR, :], z[:, j % ZR, :], h_hi[:, j % ZR, :].bitcast(F32),
                                      ALU.subtract).then_inc(lo_done, 1)
                    if j == 1 and not first:
                        combine(k - 1, E - 1, 1 - parity)
                    if j % FC == 2 and j > FC:
                        combine(k, j // FC - 1, parity)
                    for op in extra.get(j, []):
                        op()

            def final_add(b):
                dve.wait_ge(final_psum, b + 1)
                xs = x_tok[:, b * TILES:(b + 1) * TILES, :].rearrange("p t h -> p (t h)")
                dve.tensor_tensor(xs, misc[:, b % 2, :], xs, ALU.add).then_inc(final_ready, 1)

            run_slots(dve, slot)
            combine(SLOTS - 1, E - 1, 1)
            dve.wait_ge(combined, E * SLOTS)
            dve.wait_ge(added, E * SLOTS)
            for half in range(HALVES):
                at = slice((B - 1) * T + half * CH, (B - 1) * T + (half + 1) * CH)
                dve.tensor_tensor(state[:, at], state[:, at], weighted[:, E - 1, half * CH:(half + 1) * CH],
                                  ALU.add).then_inc(final_T, 1)
            for half in range(HALVES):
                dve.wait_ge(final_psum, B + half)
                t0 = (B - 1) * TILES + half * TILES // HALVES
                xs = x_tok[:, t0:t0 + TILES // HALVES, :].rearrange("p t h -> p (t h)")
                dve.tensor_tensor(xs, z[:, half, 0:CH], xs, ALU.add).then_inc(final_ready, 1)

        @block.tensor
        def _(pe):
            pe.wait_ge(consts, 2)

            def warm_up(count):
                for _ in range(count):
                    pe.transpose(z[:, ZR - 1, 0:P], ident[:], ident[:])

            def early_transpose(b):
                pe.wait_ge(xn_ready, b + 1)
                for t in range(TILES):
                    ins = pe.transpose(y[:, b, t * P:(t + 1) * P], xn_early[:, b, t, :], ident[:])
                ins.then_inc(xnT_psum, 1)

            def intake_transpose(k):
                pe.wait_ge(intake_xn, k)
                pe.wait_ge(gate_step, GATE_STEPS * (k + 1) + 2)
                for t in range(PER_SLOT):
                    ins = pe.transpose(misc[:, 1, t * P:(t + 1) * P], xn_pair[:, t, :], ident[:])
                ins.then_inc(intake_psum, 1)

            def final_transpose(b):
                pe.wait_ge(final_T, b + 1)
                if b >= 2:
                    pe.wait_ge(final_ready, b - 1)
                for t in range(TILES):
                    ins = pe.transpose(misc[:, b % 2, t * P:(t + 1) * P],
                                       state[:, b * T + t * P:b * T + (t + 1) * P], ident[:])
                ins.then_inc(final_psum, 1)

            def logits(k, rnd, parity):
                pe.wait_ge(cur_ready, k + 1)
                if isinstance(k, int) and k == 0:
                    pe.wait_ge(wg_ready, 2)
                for t in range(TILES):
                    w = wg_split[:, bass.ds(rnd, 1), :, :].rearrange("p r s e -> p (r s e)")
                    dst = misc[:, 1, t * 2 * E:(t + 1) * 2 * E]
                    pe.matmul(dst, cur_hi[:, parity, t * P:(t + 1) * P], w, start=True, stop=False)
                    ins = pe.matmul(dst, cur_lo[:, parity, t * P:(t + 1) * P], w, start=False, stop=True)
                ins.then_inc(lg_psum, 1)

            def gate_transpose(k):
                pe.wait_ge(gate_ready, k + 1)
                if isinstance(k, int) and k == 0:
                    pe.wait_ge(cols_ready, 1)
                else:
                    pe.wait_ge(gateT_ready, k)
                pe.transpose(misc[0:E * TILES, 0, 0:P], gate_w[:].rearrange("p e t -> p (e t)"),
                             ident[:]).then_inc(gateT_psum, 1)

            def up(j, parity):
                e, c = divmod(j, FC)
                hi, lo = (w[:, e, c * P:(c + 1) * P] for w in (w1_hi, w1_lo))
                dst = z[:, j % ZR, :]
                pe.matmul(dst, hi, cur_hi[:, parity, :], start=True, stop=False)
                pe.matmul(dst, hi, cur_lo[:, parity, :], start=False, stop=False)
                pe.matmul(dst, lo, cur_hi[:, parity, :], start=False, stop=True).then_inc(z_full, 1)

            def down(k, j):
                e, c = divmod(j, FC)
                pe.wait_ge(lo_done, STEPS * k + j + 1)
                if c == 0:
                    wait(pe, combined, E * k + e + 1 - YR)
                hi, lo = (w[:, e, c, :] for w in (w2_hi, w2_lo))
                dst = y[:, e % YR, :]
                pe.matmul(dst, hi, h_hi[:, j % ZR, :], start=(c == 0), stop=False)
                pe.matmul(dst, hi, h_lo[:, j % ZR, :], start=False, stop=False)
                ins = pe.matmul(dst, lo, h_hi[:, j % ZR, :], start=False, stop=(c == FC - 1))
                if c == FC - 1:
                    ins.then_inc(y_full, 1)

            warm_up(40)
            pe.wait_ge(rows_in, 48)
            pe.transpose(misc[:, 0, 0:ROWS], rows[:], ident[0:ROWS, 0:ROWS]).then_inc(cols_psum, 1)
            early_transpose(0)
            warm_up(8)
            logits(0, 0, 0)
            pe.wait_ge(w_lo, 1)
            for j in range(LAG):
                up(j, 0)
            pe.wait_ge(state_ready, 1)

            def slot(k, parity, first=False, last=False, intake=False, ahead=False):
                for j in range(STEPS):
                    if first and (j + LAG) % FC == 0 and j + LAG < STEPS:
                        pe.wait_ge(w_lo, 2 * ((j + LAG) // FC) + 1)
                    if first and j % FC == 0:
                        pe.wait_ge(w_lo, 2 * (j // FC) + 2)
                    if first and j == FC:
                        pe.wait_ge(state_ready, EARLY)
                    if j + LAG < STEPS:
                        up(j + LAG, parity)
                    elif not last:
                        up(j + LAG - STEPS, 1 - parity)
                    down(k, j)
                    if first and j == EARLY_T_AT:
                        gate_transpose(0)
                        early_transpose(1)
                    if j == 5 and not last:
                        logits(k + 1, block_of(k + 1, 1 - parity)[1], 1 - parity)
                    if j == 8 and intake:
                        intake_transpose(k)
                    if j == GATE_T_AT and not last:
                        gate_transpose(k + 1)
                    if last and FINAL_AT <= j < FINAL_AT + B - 1:
                        final_transpose(j - FINAL_AT)

            run_slots(pe, slot)
            for half in range(HALVES):
                pe.wait_ge(final_T, B + half)
                for t in range(TILES // HALVES):
                    at = (B - 1) * T + half * CH + t * P
                    ins = pe.transpose(z[:, half, t * P:(t + 1) * P], state[:, at:at + P], ident[:])
                ins.then_inc(final_psum, 1)


_INS = ['L0_attn_x', 'L0_attn_delta', 'L0_attn_alpha', 'L0_attn_beta', 'L0_attn_gamma', 'L0_attn_omega',
        'L0_ffn_Wg', 'L0_ffn_bg', 'L0_ffn_W1', 'L0_ffn_b1', 'L0_ffn_W2', 'L0_ffn_b2']
_OUTS = [((8, 512, 128), 'float32')]


def kernel(**inputs):
    import numpy as _np
    import concourse.bacc as _bacc
    from concourse import mybir as _mybir
    from concourse.bass_utils import run_bass_kernel_spmd as _run

    nc = _bacc.Bacc("TRN2", target_bir_lowering=False, num_devices=1)
    arrays, args = {}, []
    for name in _INS:
        a = _np.ascontiguousarray(inputs[name])
        arrays[f"in_{name}_dram"] = a
        args.append(nc.dram_tensor(f"in_{name}_dram", a.shape, _mybir.dt.from_np(a.dtype), kind="ExternalInput").ap())
    for i, (shape, dtype) in enumerate(_OUTS):
        dt = _mybir.dt.from_np(_np.dtype(dtype))
        args.append(nc.dram_tensor(f"out_{i}_dram", shape, dt, kind="ExternalOutput").ap())
    ema_and_routed_ffn_kernel(nc, *args)
    r = _run(nc, [arrays], core_ids=[0])
    got = tuple(r.results[0][f"out_{i}_dram"] for i in range(len(_OUTS)))
    return got[0]
```
